# Optimizing a Trainium2 kernel written in Bass

```python
import numpy as np
import jax
import jax.numpy as jnp

def _softmax(x, axis=-1):
    return jax.nn.softmax(x, axis=axis)

def _gelu(x):
    return jax.nn.gelu(x, approximate=True)

def _silu(x):
    return jax.nn.silu(x)

def _sigmoid(x):
    return jax.nn.sigmoid(x)

def _layernorm(x, axis=-1, eps=1e-05):
    m = jnp.mean(x, axis=axis, keepdims=True)
    v = jnp.var(x, axis=axis, keepdims=True)
    return (x - m) / jnp.sqrt(v + eps)

def _scatter_add(tgt, idx, src, axis=0):
    return tgt.at[idx].add(src)

def _segment_sum(src, seg, n):
    return jax.ops.segment_sum(src, seg, n)
kernel_name = 'mk_xattn_ffn_d4_seqx_r8_7cb4cf'

def setup_inputs(seed: int=0):
    np.random.seed(seed)
    _w = jnp.asarray

    def _rec_inputs():
        import jax
        import jax.numpy as jnp
        _rk = jax.random.key(seed)
        x = 7.22e-05 + 1 * jax.random.normal(jax.random.fold_in(_rk, 1), (64, 128, 128), jnp.float32)
        _lenS = 128 - jax.random.randint(jax.random.fold_in(_rk, 7), (64,), 0, max(1, 128 // 4) + 1, jnp.int32)
        _lenS2 = 120 - jax.random.randint(jax.random.fold_in(_rk, 8), (64,), 0, max(1, 120 // 4) + 1, jnp.int32)
        _ctx_1024P = jax.random.normal(jax.random.fold_in(_rk, 11), (64, 16, 128), jnp.float32)
        _ctx_1024c = jax.random.dirichlet(jax.random.fold_in(_rk, 511), 0.3 * jnp.ones((16,), jnp.float32), (64, 120))
        _ctx_1024t = jnp.einsum('bsk,bkd->bsd', _ctx_1024c, _ctx_1024P)
        _ctx_1024t = _ctx_1024t * jax.lax.rsqrt(jnp.mean(jnp.square(_ctx_1024t)) + 1e-12) * 0.953939
        ctx_1024 = 4.13588e-05 + 0.999923 * (_ctx_1024t + 0.3 * jax.random.normal(jax.random.fold_in(_rk, 611), (64, 120, 128), jnp.float32))
        _validS = jnp.arange(128)[None, :] < _lenS[:, None]
        _validS2 = jnp.arange(120)[None, :] < _lenS2[:, None]
        _causal = jnp.tril(jnp.ones((128, 128), dtype=bool))
        mask_1x1xSxS2_fk1 = jnp.where(jnp.broadcast_to(_validS2[0:1, None, None, :], (1, 1, 128, 120)), 1.0, 0.0).astype(jnp.float32)
        return (x, ctx_1024, _lenS2, mask_1x1xSxS2_fk1)
    x, ctx_1024, _lenS2, mask_1x1xSxS2_fk1 = _rec_inputs()

    def _L0_xattn_setup():
        import jax, jax.numpy as jnp
        import numpy as np
        ATT_DIM = 128
        N_HEADS = 16
        D_HEAD = ATT_DIM // N_HEADS
        LARGE = 1e+30

        def _attention(query, value, value_lens, Wq, bq, Wk, bk, Wv, bv, Wf, bf):
            B, Tq, _ = query.shape
            Tv = value.shape[1]
            k = value @ Wk + bk
            v = value @ Wv + bv
            q = (query @ Wq + bq) / jnp.sqrt(jnp.asarray(D_HEAD, query.dtype))
            q = q.reshape(B, Tq, N_HEADS, D_HEAD)
            k = k.reshape(B, Tv, N_HEADS, D_HEAD)
            v = v.reshape(B, Tv, N_HEADS, D_HEAD)
            energy = jnp.einsum('bind,bjnd->bnij', q, k)
            mask = (jnp.arange(Tv)[None, :] < value_lens[:, None]).astype(energy.dtype)
            energy = energy - (1.0 - mask)[:, None, None, :] * jnp.asarray(LARGE, energy.dtype)
            att_weight = jax.nn.softmax(energy, axis=-1)
            context = jnp.einsum('bnij,bjnd->bind', att_weight, v).reshape(B, Tq, ATT_DIM)
            return context @ Wf + bf
        key = jax.random.key(seed)
        ks = jax.random.split(key, 12)
        B, Tq, Tv, D = (4, 256, 256, 128)
        s = 1.0 / np.sqrt(D)
        sf = 1.0 / np.sqrt(ATT_DIM)
        return {'query': jax.random.normal(ks[0], (B, Tq, D), jnp.float32), 'value': jax.random.normal(ks[1], (B, Tv, D), jnp.float32), 'value_lens': jax.random.randint(ks[2], (B,), 0, Tv, jnp.int32), 'Wq': jax.random.normal(ks[3], (D, ATT_DIM), jnp.float32) * s, 'bq': jnp.zeros((ATT_DIM,), jnp.float32), 'Wk': jax.random.normal(ks[4], (D, ATT_DIM), jnp.float32) * s, 'bk': jnp.zeros((ATT_DIM,), jnp.float32), 'Wv': jax.random.normal(ks[5], (D, ATT_DIM), jnp.float32) * s, 'bv': jnp.zeros((ATT_DIM,), jnp.float32), 'Wf': jax.random.normal(ks[6], (ATT_DIM, ATT_DIM), jnp.float32) * sf, 'bf': jnp.zeros((ATT_DIM,), jnp.float32)}
    _L0_xattn_all = _L0_xattn_setup()
    _L0_xattn_in = {k: v for k, v in _L0_xattn_all.items() if k in ('Wq', 'bq', 'Wk', 'bk', 'Wv', 'bv', 'Wf', 'bf')}
    del _L0_xattn_all

    def _L0_ffn_setup():
        import jax, jax.numpy as jnp
        import numpy as np
        TOP_K = 2
        key = jax.random.key(seed)
        k1, k2, k3, k4 = jax.random.split(key, 4)
        B, S, D, F, E = (2, 256, 128, 512, 8)
        x = jax.random.normal(k1, (B, S, D), dtype=jnp.float32)
        choice = jax.random.normal(k2, (E, D), dtype=jnp.float32) / np.sqrt(D)
        W1 = jax.random.normal(k3, (E, D, F), dtype=jnp.float32) / np.sqrt(D)
        W2 = jax.random.normal(k4, (E, F, D), dtype=jnp.float32) / np.sqrt(F)
        return {'x': x, 'choice': choice, 'W1': W1, 'W2': W2}
    _L0_ffn_all = _L0_ffn_setup()
    _L0_ffn_in = {k: v for k, v in _L0_ffn_all.items() if k in ('choice', 'W1', 'W2')}
    del _L0_ffn_all

    def _L1_xattn_setup():
        import jax, jax.numpy as jnp
        import numpy as np
        EMBED = 128
        HEADS = 16
        HIDDEN = 128
        HEAD_DIM = EMBED // HEADS
        key = jax.random.key(seed)
        ks = jax.random.split(key, 9)
        s = 1.0 / np.sqrt(HIDDEN)
        return {'q': jax.random.normal(ks[0], (2, 256, HIDDEN), jnp.float32), 'k': jax.random.normal(ks[1], (2, 256, HIDDEN), jnp.float32), 'v': jax.random.normal(ks[2], (2, 256, HIDDEN), jnp.float32), 'wq': jax.random.normal(ks[3], (HIDDEN, EMBED), jnp.float32) * s, 'bq': jax.random.normal(ks[4], (EMBED,), jnp.float32) * s, 'wk': jax.random.normal(ks[5], (HIDDEN, EMBED), jnp.float32) * s, 'bk': jax.random.normal(ks[6], (EMBED,), jnp.float32) * s, 'wv': jax.random.normal(ks[7], (HIDDEN, EMBED), jnp.float32) * s, 'bv': jax.random.normal(ks[8], (EMBED,), jnp.float32) * s}
    _L1_xattn_all = _L1_xattn_setup()
    _L1_xattn_in = {k: v for k, v in _L1_xattn_all.items() if k in ('wq', 'bq', 'wk', 'bk', 'wv', 'bv')}
    del _L1_xattn_all

    def _L1_ffn_setup():
        import jax, jax.numpy as jnp
        import numpy as np
        QMAX = 127.0

        def _ste_round(v):
            return v + jax.lax.stop_gradient(jnp.round(v) - v)

        def _act_fake_quant(x, clip_factor):
            scale = jax.nn.sigmoid(clip_factor) * jnp.max(jnp.abs(x)) / QMAX
            return jnp.clip(_ste_round(x / scale), -QMAX - 1.0, QMAX) * scale

        def _weight_fake_quant(w):
            scale = jnp.max(jnp.abs(w), axis=1, keepdims=True) / QMAX
            return jnp.clip(_ste_round(w / scale), -QMAX - 1.0, QMAX) * scale
        key = jax.random.key(seed)
        k1, k2, k3, k4 = jax.random.split(key, 4)
        B, S, H, I = (8, 1024, 128, 352)
        return {'x': jax.random.normal(k1, (B, S, H), dtype=jnp.float32), 'clip_x': jnp.full((1,), 4.0, dtype=jnp.float32), 'clip_down': jnp.full((1,), 4.0, dtype=jnp.float32), 'w_gate': jax.random.normal(k2, (I, H), dtype=jnp.float32) * 0.02, 'w_up': jax.random.normal(k3, (I, H), dtype=jnp.float32) * 0.02, 'w_down': jax.random.normal(k4, (H, I), dtype=jnp.float32) * 0.02}
    _L1_ffn_all = _L1_ffn_setup()
    _L1_ffn_in = {k: v for k, v in _L1_ffn_all.items() if k in ('clip_x', 'clip_down', 'w_gate', 'w_up', 'w_down')}
    del _L1_ffn_all

    def _L2_xattn_setup():
        import jax, jax.numpy as jnp
        import numpy as np
        D_MODEL = 128
        NUM_HEADS = 16
        DEPTH = D_MODEL // NUM_HEADS
        B, S = (4, 256)

        def _split_heads(x):
            b, s, _ = x.shape
            return x.reshape(b, s, NUM_HEADS, DEPTH).transpose(0, 2, 1, 3)
        key = jax.random.key(seed)
        ks = jax.random.split(key, 12)
        scale = 1.0 / np.sqrt(D_MODEL)
        inp = {'q': jax.random.normal(ks[0], (B, S, D_MODEL), jnp.float32), 'k': jax.random.normal(ks[1], (B, S, D_MODEL), jnp.float32), 'v': jax.random.normal(ks[2], (B, S, D_MODEL), jnp.float32), 'mask': jnp.triu(jnp.ones((S, S), jnp.float32), k=1)[None, None, :, :], 'wq': jax.random.normal(ks[3], (D_MODEL, D_MODEL), jnp.float32) * scale, 'bq': jnp.zeros((D_MODEL,), jnp.float32), 'wk': jax.random.normal(ks[4], (D_MODEL, D_MODEL), jnp.float32) * scale, 'bk': jnp.zeros((D_MODEL,), jnp.float32), 'wv': jax.random.normal(ks[5], (D_MODEL, D_MODEL), jnp.float32) * scale, 'bv': jnp.zeros((D_MODEL,), jnp.float32), 'wo': jax.random.normal(ks[6], (D_MODEL, D_MODEL), jnp.float32) * scale, 'bo': jnp.zeros((D_MODEL,), jnp.float32)}
        return inp
    _L2_xattn_all = _L2_xattn_setup()
    _L2_xattn_in = {k: v for k, v in _L2_xattn_all.items() if k in ('wq', 'bq', 'wk', 'bk', 'wv', 'bv', 'wo', 'bo')}
    del _L2_xattn_all

    def _L2_ffn_setup():
        import jax, jax.numpy as jnp
        import numpy as np
        D_MODEL = 128
        DEPTH = 8
        M = 2 ** DEPTH
        N_INTERNAL = M - 1
        B, T = (8, 512)

        def _leaf_probs(gate):
            BT = gate.shape[0]
            lp = jnp.ones((BT, M), dtype=gate.dtype)
            for level in range(DEPTH):
                n = 2 ** level
                half = M // (2 * n)
                g = gate[:, n - 1:2 * n - 1]
                f = jnp.stack([1.0 - g, g], axis=-1)
                f = jnp.broadcast_to(f[..., None], (BT, n, 2, half))
                lp = lp * f.reshape(BT, M)
            return lp
        key = jax.random.key(seed)
        ks = jax.random.split(key, 7)
        x = jax.random.normal(ks[0], (B, T, D_MODEL), dtype=jnp.float32)
        Wq = jax.random.normal(ks[1], (D_MODEL, D_MODEL), dtype=jnp.float32) * 0.02
        routers = jax.random.normal(ks[2], (N_INTERNAL, D_MODEL), dtype=jnp.float32) * 0.02
        leaf_keys = jax.random.normal(ks[3], (M, D_MODEL), dtype=jnp.float32) * 0.02
        leaf_values = jax.random.normal(ks[4], (M, D_MODEL), dtype=jnp.float32) * 0.02
        Wout_w = jax.random.normal(ks[5], (D_MODEL, D_MODEL), dtype=jnp.float32) * 0.02
        Wout_b = jax.random.normal(ks[6], (D_MODEL,), dtype=jnp.float32) * 0.02
        return {'x': x, 'Wq': Wq, 'routers': routers, 'leaf_keys': leaf_keys, 'leaf_values': leaf_values, 'Wout_w': Wout_w, 'Wout_b': Wout_b}
    _L2_ffn_all = _L2_ffn_setup()
    _L2_ffn_in = {k: v for k, v in _L2_ffn_all.items() if k in ('Wq', 'routers', 'leaf_keys', 'leaf_values', 'Wout_w', 'Wout_b')}
    del _L2_ffn_all

    def _L3_xattn_setup():
        import jax, jax.numpy as jnp
        import numpy as np
        N_HEAD = 16

        def _split_heads(t):
            B, L, D = t.shape
            return t.reshape(B, L, N_HEAD, D // N_HEAD).transpose(0, 2, 1, 3)
        key = jax.random.key(seed)
        ks = jax.random.split(key, 6)
        B, S, T, D = (4, 128, 72, 128)
        std = 0.02
        return {'x': jax.random.normal(ks[0], (B, S, D), jnp.float32), 'encoder_output': jax.random.normal(ks[1], (B, T, D), jnp.float32), 'w_attn': jax.random.normal(ks[2], (D, 3 * D), jnp.float32) * std, 'b_attn': jnp.zeros((3 * D,), jnp.float32), 'w_vis': jax.random.normal(ks[3], (D, D), jnp.float32) * std, 'b_vis': jnp.zeros((D,), jnp.float32), 'w_proj': jax.random.normal(ks[4], (D, D), jnp.float32) * std, 'b_proj': jnp.zeros((D,), jnp.float32)}
    _L3_xattn_all = _L3_xattn_setup()
    _L3_xattn_in = {k: v for k, v in _L3_xattn_all.items() if k in ('w_attn', 'b_attn', 'w_vis', 'b_vis', 'w_proj', 'b_proj')}
    del _L3_xattn_all

    def _L3_ffn_setup():
        import jax, jax.numpy as jnp
        import numpy as np
        DIM = 128

        def _reference_tuple_inner(x, W_r, W_k, W_v, mu_r, mu_k):
            B, T, C = x.shape
            x_prev = jnp.concatenate([jnp.zeros((B, 1, C), x.dtype), x[:, :-1, :]], axis=1)
            xr = mu_r * x + (1.0 - mu_r) * x_prev
            xk = mu_k * x + (1.0 - mu_k) * x_prev
            r = jax.nn.sigmoid(jnp.einsum('btc,dc->btd', xr, W_r))
            k = jnp.einsum('btc,dc->btd', xk, W_k)
            k_act = jnp.square(jax.nn.relu(k))
            out = r * jnp.einsum('btc,dc->btd', k_act, W_v)
            new_state = x[:, -1, :]
            return (out, new_state)
        key = jax.random.key(seed)
        ks = jax.random.split(key, 6)
        B, T, C = (8, 256, DIM)
        x = jax.random.normal(ks[0], (B, T, C), dtype=jnp.float32)
        s = 1.0 / np.sqrt(C)
        W_r = jax.random.uniform(ks[1], (C, C), jnp.float32, -s, s)
        W_k = jax.random.uniform(ks[2], (C, C), jnp.float32, -s, s)
        W_v = jax.random.uniform(ks[3], (C, C), jnp.float32, -s, s)
        mu_r = jax.random.uniform(ks[4], (C,), jnp.float32)
        mu_k = jax.random.uniform(ks[5], (C,), jnp.float32)
        return {'x': x, 'W_r': W_r, 'W_k': W_k, 'W_v': W_v, 'mu_r': mu_r, 'mu_k': mu_k}
    _L3_ffn_all = _L3_ffn_setup()
    _L3_ffn_in = {k: v for k, v in _L3_ffn_all.items() if k in ('W_r', 'W_k', 'W_v', 'mu_r', 'mu_k')}
    del _L3_ffn_all
    return {'x': x, 'ctx_1024': ctx_1024, '_lenS2': _lenS2, 'mask_1x1xSxS2_fk1': mask_1x1xSxS2_fk1, 'L0_xattn_Wq': _L0_xattn_in['Wq'], 'L0_xattn_bq': _L0_xattn_in['bq'], 'L0_xattn_Wk': _L0_xattn_in['Wk'], 'L0_xattn_bk': _L0_xattn_in['bk'], 'L0_xattn_Wv': _L0_xattn_in['Wv'], 'L0_xattn_bv': _L0_xattn_in['bv'], 'L0_xattn_Wf': _L0_xattn_in['Wf'], 'L0_xattn_bf': _L0_xattn_in['bf'], 'L0_ffn_choice': _L0_ffn_in['choice'], 'L0_ffn_W1': _L0_ffn_in['W1'], 'L0_ffn_W2': _L0_ffn_in['W2'], 'L1_xattn_wq': _L1_xattn_in['wq'], 'L1_xattn_bq': _L1_xattn_in['bq'], 'L1_xattn_wk': _L1_xattn_in['wk'], 'L1_xattn_bk': _L1_xattn_in['bk'], 'L1_xattn_wv': _L1_xattn_in['wv'], 'L1_xattn_bv': _L1_xattn_in['bv'], 'L1_ffn_clip_x': _L1_ffn_in['clip_x'], 'L1_ffn_clip_down': _L1_ffn_in['clip_down'], 'L1_ffn_w_gate': _L1_ffn_in['w_gate'], 'L1_ffn_w_up': _L1_ffn_in['w_up'], 'L1_ffn_w_down': _L1_ffn_in['w_down'], 'L2_xattn_wq': _L2_xattn_in['wq'], 'L2_xattn_bq': _L2_xattn_in['bq'], 'L2_xattn_wk': _L2_xattn_in['wk'], 'L2_xattn_bk': _L2_xattn_in['bk'], 'L2_xattn_wv': _L2_xattn_in['wv'], 'L2_xattn_bv': _L2_xattn_in['bv'], 'L2_xattn_wo': _L2_xattn_in['wo'], 'L2_xattn_bo': _L2_xattn_in['bo'], 'L2_ffn_Wq': _L2_ffn_in['Wq'], 'L2_ffn_routers': _L2_ffn_in['routers'], 'L2_ffn_leaf_keys': _L2_ffn_in['leaf_keys'], 'L2_ffn_leaf_values': _L2_ffn_in['leaf_values'], 'L2_ffn_Wout_w': _L2_ffn_in['Wout_w'], 'L2_ffn_Wout_b': _L2_ffn_in['Wout_b'], 'L3_xattn_w_attn': _L3_xattn_in['w_attn'], 'L3_xattn_b_attn': _L3_xattn_in['b_attn'], 'L3_xattn_w_vis': _L3_xattn_in['w_vis'], 'L3_xattn_b_vis': _L3_xattn_in['b_vis'], 'L3_xattn_w_proj': _L3_xattn_in['w_proj'], 'L3_xattn_b_proj': _L3_xattn_in['b_proj'], 'L3_ffn_W_r': _L3_ffn_in['W_r'], 'L3_ffn_W_k': _L3_ffn_in['W_k'], 'L3_ffn_W_v': _L3_ffn_in['W_v'], 'L3_ffn_mu_r': _L3_ffn_in['mu_r'], 'L3_ffn_mu_k': _L3_ffn_in['mu_k']}

def reference(x, ctx_1024, _lenS2, mask_1x1xSxS2_fk1, L0_xattn_Wq, L0_xattn_bq, L0_xattn_Wk, L0_xattn_bk, L0_xattn_Wv, L0_xattn_bv, L0_xattn_Wf, L0_xattn_bf, L0_ffn_choice, L0_ffn_W1, L0_ffn_W2, L1_xattn_wq, L1_xattn_bq, L1_xattn_wk, L1_xattn_bk, L1_xattn_wv, L1_xattn_bv, L1_ffn_clip_x, L1_ffn_clip_down, L1_ffn_w_gate, L1_ffn_w_up, L1_ffn_w_down, L2_xattn_wq, L2_xattn_bq, L2_xattn_wk, L2_xattn_bk, L2_xattn_wv, L2_xattn_bv, L2_xattn_wo, L2_xattn_bo, L2_ffn_Wq, L2_ffn_routers, L2_ffn_leaf_keys, L2_ffn_leaf_values, L2_ffn_Wout_w, L2_ffn_Wout_b, L3_xattn_w_attn, L3_xattn_b_attn, L3_xattn_w_vis, L3_xattn_b_vis, L3_xattn_w_proj, L3_xattn_b_proj, L3_ffn_W_r, L3_ffn_W_k, L3_ffn_W_v, L3_ffn_mu_r, L3_ffn_mu_k):
    import jax
    import jax.numpy as jnp

    def _L0_xattn_ref(query, value, value_lens, Wq, bq, Wk, bk, Wv, bv, Wf, bf):
        import jax, jax.numpy as jnp
        import numpy as np
        ATT_DIM = 128
        N_HEADS = 16
        D_HEAD = ATT_DIM // N_HEADS
        LARGE = 1e+30

        def _attention(query, value, value_lens, Wq, bq, Wk, bk, Wv, bv, Wf, bf):
            B, Tq, _ = query.shape
            Tv = value.shape[1]
            k = value @ Wk + bk
            v = value @ Wv + bv
            q = (query @ Wq + bq) / jnp.sqrt(jnp.asarray(D_HEAD, query.dtype))
            q = q.reshape(B, Tq, N_HEADS, D_HEAD)
            k = k.reshape(B, Tv, N_HEADS, D_HEAD)
            v = v.reshape(B, Tv, N_HEADS, D_HEAD)
            energy = jnp.einsum('bind,bjnd->bnij', q, k)
            mask = (jnp.arange(Tv)[None, :] < value_lens[:, None]).astype(energy.dtype)
            energy = energy - (1.0 - mask)[:, None, None, :] * jnp.asarray(LARGE, energy.dtype)
            att_weight = jax.nn.softmax(energy, axis=-1)
            context = jnp.einsum('bnij,bjnd->bind', att_weight, v).reshape(B, Tq, ATT_DIM)
            return context @ Wf + bf
        return _attention(query, value, value_lens, Wq, bq, Wk, bk, Wv, bv, Wf, bf)

    def _L0_ffn_ref(x, choice, W1, W2):
        import jax, jax.numpy as jnp
        import numpy as np
        TOP_K = 2
        B, S, D = x.shape
        E = choice.shape[0]
        logits = jnp.einsum('bsd,ed->bse', x, choice)
        weights = jax.nn.softmax(logits, axis=-1)
        k_w, k_idx = jax.lax.top_k(weights, TOP_K)
        cw = jnp.sum(jax.nn.one_hot(k_idx, E, dtype=x.dtype) * k_w[..., None], axis=-2)
        xt = x.reshape(B * S, D)
        cwt = cw.reshape(B * S, E)
        y = jnp.zeros_like(xt)
        for e in range(E):
            h = jax.nn.silu(xt @ W1[e]) @ W2[e]
            y = y + cwt[:, e:e + 1] * h
        return y.reshape(B, S, D)

    def _L1_xattn_ref(q, k, v, wq, bq, wk, bk, wv, bv):
        import jax, jax.numpy as jnp
        import numpy as np
        EMBED = 128
        HEADS = 16
        HIDDEN = 128
        HEAD_DIM = EMBED // HEADS
        B = q.shape[0]

        def split_heads(x):
            return x.reshape(B, -1, HEADS, HEAD_DIM).transpose(0, 2, 1, 3)
        qh = split_heads(q @ wq + bq)
        kh = split_heads(k @ wk + bk)
        vh = split_heads(v @ wv + bv)
        scale = 1.0 / np.sqrt(HEAD_DIM).astype(np.float32)
        scores = jnp.einsum('bhqd,bhkd->bhqk', qh, kh) * scale
        probs = jax.nn.softmax(scores, axis=-1)
        out = jnp.einsum('bhqk,bhkd->bhqd', probs, vh)
        return out.transpose(0, 2, 1, 3).reshape(B, -1, EMBED)

    def _L1_ffn_ref(x, clip_x, clip_down, w_gate, w_up, w_down):
        import jax, jax.numpy as jnp
        import numpy as np
        QMAX = 127.0

        def _ste_round(v):
            return v + jax.lax.stop_gradient(jnp.round(v) - v)

        def _act_fake_quant(x, clip_factor):
            scale = jax.nn.sigmoid(clip_factor) * jnp.max(jnp.abs(x)) / QMAX
            return jnp.clip(_ste_round(x / scale), -QMAX - 1.0, QMAX) * scale

        def _weight_fake_quant(w):
            scale = jnp.max(jnp.abs(w), axis=1, keepdims=True) / QMAX
            return jnp.clip(_ste_round(w / scale), -QMAX - 1.0, QMAX) * scale
        xq = _act_fake_quant(x, clip_x[0])
        gate = jnp.einsum('bsh,ih->bsi', xq, _weight_fake_quant(w_gate))
        up = jnp.einsum('bsh,ih->bsi', xq, _weight_fake_quant(w_up))
        h = _act_fake_quant(jax.nn.silu(gate) * up, clip_down[0])
        return jnp.einsum('bsi,hi->bsh', h, _weight_fake_quant(w_down))

    def _L2_xattn_ref(q, k, v, mask, wq, bq, wk, bk, wv, bv, wo, bo):
        import jax, jax.numpy as jnp
        import numpy as np
        D_MODEL = 128
        NUM_HEADS = 16
        DEPTH = D_MODEL // NUM_HEADS
        B, S = (4, 256)

        def _split_heads(x):
            b, s, _ = x.shape
            return x.reshape(b, s, NUM_HEADS, DEPTH).transpose(0, 2, 1, 3)
        qh = _split_heads(q @ wq + bq)
        kh = _split_heads(k @ wk + bk)
        vh = _split_heads(v @ wv + bv)
        inv_sqrt_dk = 1.0 / jnp.sqrt(jnp.asarray(DEPTH, jnp.float32))
        logits = jnp.einsum('bhqd,bhkd->bhqk', qh, kh) * inv_sqrt_dk
        logits = logits + mask * -1000000000.0
        attn = jax.nn.softmax(logits, axis=-1)
        out = jnp.einsum('bhqk,bhkd->bhqd', attn, vh)
        out = out.transpose(0, 2, 1, 3).reshape(q.shape[0], -1, D_MODEL)
        return out @ wo + bo

    def _L2_ffn_ref(x, Wq, routers, leaf_keys, leaf_values, Wout_w, Wout_b):
        import jax, jax.numpy as jnp
        import numpy as np
        D_MODEL = 128
        DEPTH = 8
        M = 2 ** DEPTH
        N_INTERNAL = M - 1
        B, T = (8, 512)

        def _leaf_probs(gate):
            BT = gate.shape[0]
            lp = jnp.ones((BT, M), dtype=gate.dtype)
            for level in range(DEPTH):
                n = 2 ** level
                half = M // (2 * n)
                g = gate[:, n - 1:2 * n - 1]
                f = jnp.stack([1.0 - g, g], axis=-1)
                f = jnp.broadcast_to(f[..., None], (BT, n, 2, half))
                lp = lp * f.reshape(BT, M)
            return lp
        Bv, Tv, d = x.shape
        q = jnp.einsum('btd,ed->bte', x, Wq)
        q_flat = q.reshape(Bv * Tv, d)
        gate = jax.nn.sigmoid(q_flat @ routers.T)
        leaf_prob = _leaf_probs(gate)
        ret = (leaf_prob @ leaf_values).reshape(Bv, Tv, d)
        return jnp.einsum('btd,ed->bte', ret, Wout_w) + Wout_b

    def _L3_xattn_ref(x, encoder_output, w_attn, b_attn, w_vis, b_vis, w_proj, b_proj):
        import jax, jax.numpy as jnp
        import numpy as np
        N_HEAD = 16

        def _split_heads(t):
            B, L, D = t.shape
            return t.reshape(B, L, N_HEAD, D // N_HEAD).transpose(0, 2, 1, 3)
        B, S, D = x.shape
        qkv = x @ w_attn + b_attn
        q = _split_heads(qkv[..., :D])
        enc = encoder_output @ w_vis + b_vis
        kv = _split_heads(enc)
        dh = D // N_HEAD
        w = jnp.einsum('bhsd,bhtd->bhst', q, kv) / jnp.sqrt(jnp.float32(dh))
        w = jax.nn.softmax(w, axis=-1)
        a = jnp.einsum('bhst,bhtd->bhsd', w, kv)
        a = a.transpose(0, 2, 1, 3).reshape(B, S, D)
        out = a @ w_proj + b_proj
        return out

    def _L3_ffn_ref(x, W_r, W_k, W_v, mu_r, mu_k):
        import jax, jax.numpy as jnp
        import numpy as np
        DIM = 128

        def _reference_tuple_inner(x, W_r, W_k, W_v, mu_r, mu_k):
            B, T, C = x.shape
            x_prev = jnp.concatenate([jnp.zeros((B, 1, C), x.dtype), x[:, :-1, :]], axis=1)
            xr = mu_r * x + (1.0 - mu_r) * x_prev
            xk = mu_k * x + (1.0 - mu_k) * x_prev
            r = jax.nn.sigmoid(jnp.einsum('btc,dc->btd', xr, W_r))
            k = jnp.einsum('btc,dc->btd', xk, W_k)
            k_act = jnp.square(jax.nn.relu(k))
            out = r * jnp.einsum('btc,dc->btd', k_act, W_v)
            new_state = x[:, -1, :]
            return (out, new_state)
        return _reference_tuple_inner(x, W_r, W_k, W_v, mu_r, mu_k)[0]
    x = x + _L0_xattn_ref(_layernorm(x, axis=-1), ctx_1024, _lenS2, L0_xattn_Wq, L0_xattn_bq, L0_xattn_Wk, L0_xattn_bk, L0_xattn_Wv, L0_xattn_bv, L0_xattn_Wf, L0_xattn_bf)
    x = x + _L0_ffn_ref(_layernorm(x, axis=-1), L0_ffn_choice, L0_ffn_W1, L0_ffn_W2)
    x = x + _L1_xattn_ref(_layernorm(x, axis=-1), ctx_1024, ctx_1024, L1_xattn_wq, L1_xattn_bq, L1_xattn_wk, L1_xattn_bk, L1_xattn_wv, L1_xattn_bv)
    x = x + _L1_ffn_ref(_layernorm(x, axis=-1), L1_ffn_clip_x, L1_ffn_clip_down, L1_ffn_w_gate, L1_ffn_w_up, L1_ffn_w_down)
    x = x + _L2_xattn_ref(_layernorm(x, axis=-1), ctx_1024, ctx_1024, mask_1x1xSxS2_fk1, L2_xattn_wq, L2_xattn_bq, L2_xattn_wk, L2_xattn_bk, L2_xattn_wv, L2_xattn_bv, L2_xattn_wo, L2_xattn_bo)
    x = x + _L2_ffn_ref(_layernorm(x, axis=-1), L2_ffn_Wq, L2_ffn_routers, L2_ffn_leaf_keys, L2_ffn_leaf_values, L2_ffn_Wout_w, L2_ffn_Wout_b)
    x = x + _L3_xattn_ref(_layernorm(x, axis=-1), ctx_1024, L3_xattn_w_attn, L3_xattn_b_attn, L3_xattn_w_vis, L3_xattn_b_vis, L3_xattn_w_proj, L3_xattn_b_proj)
    x = x + _L3_ffn_ref(_layernorm(x, axis=-1), L3_ffn_W_r, L3_ffn_W_k, L3_ffn_W_v, L3_ffn_mu_r, L3_ffn_mu_k)
    return x

_drawn_inputs = setup_inputs


def setup_inputs(seed=0):
    import zlib

    import numpy as np

    out = dict(_drawn_inputs(seed))
    spreads = {'L0_xattn_bq': (0.0, 0.359),
     'L0_xattn_bk': (0.0, 2.0),
     'L0_xattn_bv': (0.0, 0.1),
     'L0_xattn_bf': (0.0, 0.1),
     'L2_xattn_bq': (0.0, 1.843),
     'L2_xattn_bk': (0.0, 2.0),
     'L2_xattn_bv': (0.0, 0.504),
     'L2_xattn_bo': (0.0, 0.498),
     'L3_xattn_b_attn': (0.0, 2.0),
     'L3_xattn_b_vis': (0.0, 0.593),
     'L3_xattn_b_proj': (0.0, 0.517)}
    factors = {'L1_xattn_bq': 4.487,
     'L1_xattn_bk': 64.0,
     'L1_ffn_w_gate': 8.0,
     'L1_ffn_w_up': 8.0,
     'L1_ffn_w_down': 8.0,
     'L2_ffn_Wq': 27.772,
     'L2_ffn_routers': 27.972,
     'L2_ffn_leaf_values': 27.624,
     'L2_ffn_Wout_w': 27.382,
     'L2_ffn_Wout_b': 17.819,
     'L3_xattn_w_attn': 8.0,
     'L3_xattn_w_vis': 3.759,
     'L3_xattn_w_proj': 2.93,
     'L3_ffn_W_r': 18.339,
     'L3_ffn_mu_r': 55.001,
     'L3_ffn_W_k': 3.488,
     'L3_ffn_W_v': 3.197,
     'L3_ffn_mu_k': 6.161}
    for name, (base, spread) in spreads.items():
        noise = np.random.default_rng([zlib.crc32(name.encode()), seed]).standard_normal(out[name].shape)
        drawn = base * np.exp(spread * noise) if base else spread * noise
        out[name] = jnp.asarray(drawn.astype(out[name].dtype))
    for name, factor in factors.items():
        out[name] = (out[name] * factor).astype(out[name].dtype)
    return out
```

```python
from contextlib import ExitStack

import numpy as np
import concourse.bass as bass
from concourse import mybir

F32 = mybir.dt.float32
F16 = mybir.dt.float16
BF16 = mybir.dt.bfloat16
I32 = mybir.dt.int32
ALU = mybir.AluOpType
ACT = mybir.ActivationFunctionType
AX = mybir.AxisListType

P = 128
NB = 64
TK = 120
D = 128
HEADS = 16
DH = D // HEADS
PART = 4
GB = 4
NG = NB // GB
SLOTS = GB * PART
GT = GB * P
GK = GB * TK
E = 8
FC = 4
I1 = 352
IC = [(0, 128), (128, 128), (256, 96)]
LEAVES = 256
BIG = 998244352.0
MAGIC = 12582912.0
EPS = 1e-5
QMAX = 127.0

PACK = {}
PACK_COLS = 0
for _name, _n in ([(f"w{k}{l}", D) for l in range(4) for k in "qkv"] + [(f"wo{l}", D) for l in (0, 2, 3)]
                  + [(f"b{k}{l}", 1) for l in range(4) for k in "qkv"]
                  + [("choice", E), ("gate", 3 * D), ("up", 3 * D), ("down", 3 * P), ("tree_q", D),
                     ("routers", LEAVES), ("leaves", LEAVES), ("tree_out", D), ("mix_r", D), ("mix_k", D),
                     ("mix_v", D), ("mu_r", 1), ("mu_k", 1)]):
    PACK[_name] = (PACK_COLS, _n)
    PACK_COLS += _n
ROWS = {"bf0": (0, D), "bv1": (D, D), "bo2": (2 * D, D), "bp3": (3 * D, D), "tree_b": (4 * D, D),
        "clip_x": (5 * D, 1), "clip_down": (5 * D + 1, 1)}
ROW_COLS = 5 * D + 2


def wait(eng, sem, value):
    if isinstance(value, int) and value <= 0:
        return
    eng.wait_ge(sem, value)


def apart(eng, C):
    eng.sem_inc(C.passed, 1)


def over_groups(eng, body):
    body(0, 0, True, False)
    body(1, 1, False, False)
    with eng.Fori(0, (NG - 4) // 2) as i:
        body(i * 2 + 2, 0, False, False)
        body(i * 2 + 3, 1, False, False)
    body(NG - 2, (NG - 2) % 2, False, False)
    body(NG - 1, (NG - 1) % 2, False, True)


class Chip:
    pass


class Phase:

    def __init__(self, nc, name):
        self.nc, self.name, self.stack, self.sems = nc, name, ExitStack(), []

    def __enter__(self):
        self.stack.__enter__()
        return self

    def __exit__(self, *a):
        self.nc.clear_and_free_semaphores(self.sems)
        self.nc.all_engine_barrier()
        return self.stack.__exit__(*a)

    def sb(self, name, shape, dt=F32):
        return self.stack.enter_context(self.nc.sbuf_tensor(f"{self.name}_{name}", shape, dt))

    def sem(self, name):
        self.sems.append(self.nc.alloc_semaphore(f"{self.name}_{name}"))
        return self.sems[-1]


class Chain:

    def __init__(self, eng, sem):
        self.eng, self.sem, self.n = eng, sem, 0

    def __call__(self, ins):
        self.n += 1
        ins.then_inc(self.sem, 1)
        self.eng.wait_ge(self.sem, self.n)


def batch(t, b, n=1):
    return bass.ds(t * GB + b, n)



def norm_vector(nc, C, dve, ph):
    ch = Chain(dve, ph["norm_step"])
    st = C.stats
    t = C.norm_tmp
    ch(nc.vector.tensor_tensor(t[:, 0], st[:, :, 1], st[:, :, 4], ALU.add))
    ch(nc.vector.tensor_tensor(t[:, 1], st[:, :, 1], st[:, :, 4], ALU.subtract))
    ch(nc.vector.tensor_tensor(t[:, 2], st[:, :, 2], st[:, :, 5], ALU.add))
    ch(nc.vector.tensor_tensor(t[:, 1], t[:, 1], t[:, 1], ALU.mult))
    ch(nc.vector.scalar_tensor_tensor(out=t[:, 2], in0=t[:, 1], scalar=D / 4.0, in1=t[:, 2], op0=ALU.mult, op1=ALU.add))
    nc.vector.tensor_scalar(t[:, 1], t[:, 2], 1.0 / D, EPS, ALU.mult, ALU.add).then_inc(ph["var_ready"], 1)
    dve.wait_ge(ph["rstd_ready"], 1)
    ch(nc.vector.scalar_tensor_tensor(out=C.shift[:], in0=t[:, 0], scalar=-0.5, in1=C.rstd[:], op0=ALU.mult, op1=ALU.mult))


def norm_pool(nc, C, pool, ph):
    pool.wait_ge(ph["var_ready"], 1)
    nc.gpsimd.tensor_tensor(C.rstd[:], C.norm_tmp[:, 1], C.minus_half[:], ALU.pow).then_inc(ph["rstd_ready"], 1)


def norm_sems(ph):
    return {n: ph.sem(n) for n in ("norm_step", "var_ready", "rstd_ready")}


def normalized(nc, C, out, n):
    for b in range(GB):
        last = nc.vector.tensor_scalar(out[:, b:b + 1, :], C.x[:, batch(n, b), :], C.rstd[:, batch(n, b)],
                                       C.shift[:, batch(n, b)], ALU.mult, ALU.add)
    return last



def setup(nc, C, A):
    with Phase(nc, "setup") as ph:
        x_in, ctx_in, pack_in, rows_in, w_in, len_in, mask_in = (
            ph.sem(n) for n in ("x_in", "ctx_in", "pack_in", "rows_in", "w_in", "len_in", "mask_in"))
        pool_step, dve_step, made, folded_ready, psum_ready, psum_read, quantized = (
            ph.sem(n) for n in ("pool_step", "dve_step", "made", "folded_ready", "psum_ready", "psum_read", "quantized"))
        lens_i = ph.sb("lens_i", [P, NB], I32)
        lens = ph.sb("lens", [P, NB])
        len0 = ph.sb("len0", [P, NB])
        key_col = ph.sb("key_col", [P, 1])
        mask_f = ph.sb("mask_f", [P, TK])
        lowest = ph.sb("lowest", [P, 1])
        ones = ph.sb("ones", [P, P])
        wabs = ph.sb("wabs", [P, 9])
        wscale = ph.sb("wscale", [P, 9])
        winv = ph.sb("winv", [P, 9])
        wint = ph.sb("wint", [P, 9, D])
        diag = ph.sb("diag", [P, P])
        nx = 4
        with nc.Block() as block:

            @block.sync
            def _(sp):
                sp.dma_start(C.pack[:], A["pack"]).then_inc(pack_in, 16)
                sp.dma_start(C.rows[:], A["rows"].to_broadcast([P, ROW_COLS])).then_inc(rows_in, 16)
                sp.dma_start(lens_i[:], A["lens"].to_broadcast([P, NB])).then_inc(len_in, 16)
                sp.dma_start(mask_f[:], A["mask"]).then_inc(mask_in, 16)
                for k in range(nx):
                    s = slice(k * NB // nx, (k + 1) * NB // nx)
                    sp.dma_start(C.x[:, s, :], A["x"][:, s, :]).then_inc(x_in, 16)

            @block.gpsimd
            def _(pool):
                ch = Chain(pool, pool_step)

                def keep_where(t, value, pattern, base, cm, op):
                    ch(nc.gpsimd.affine_select(out=t, in_=t, compare_op=op, fill=value, base=base,
                                               pattern=pattern, channel_multiplier=cm))
                for t, v in ((C.ident, 1.0), (C.neg_ident, -1.0), (C.neg_big, -BIG), (C.pos_big, BIG)):
                    ch(nc.gpsimd.memset(t[:], v))
                    keep_where(t[:], 0.0, [[-1, P]], 0, 1, ALU.is_equal)
                ch(nc.gpsimd.memset(C.head_rows[:], 1.0))
                for p in range(PART):
                    t = C.head_rows[32 * p:32 * p + 32, :]
                    keep_where(t, 0.0, [[-DH, PART]], 0, 1, ALU.is_ge)
                    keep_where(t, 0.0, [[DH, PART]], DH - 1, -1, ALU.is_ge)
                ch(nc.gpsimd.memset(C.head_cols[:], 1.0))
                keep_where(C.head_cols[:], 0.0, [[-DH, PART], [1, 32]], 0, 0, ALU.is_ge)
                keep_where(C.head_cols[:], 0.0, [[DH, PART], [-1, 32]], DH - 1, 0, ALU.is_ge)
                ch(nc.gpsimd.memset(ones[:], 1.0))
                ch(nc.gpsimd.memset(C.minus_half[:], -0.5))
                ch(nc.gpsimd.iota(C.key_row[:], pattern=[[1, TK]], base=0, channel_multiplier=0,
                                  allow_small_or_imprecise_dtypes=True))
                ch(nc.gpsimd.iota(key_col[:], pattern=[[0, 1]], base=0, channel_multiplier=1,
                                  allow_small_or_imprecise_dtypes=True))
                pool.sem_inc(made, 1)

            @block.vector
            def _(dve):
                ch = Chain(dve, dve_step)
                v = nc.vector
                dve.wait_ge(len_in, 16)
                dve.wait_ge(made, 1)
                ch(v.tensor_copy(lens[:], lens_i[:]))
                ch(v.tensor_scalar(len0[:], lens[:], 0.0, None, ALU.is_gt))
                ch(v.tensor_copy(C.keep0[:], len0[:]))
                ch(v.tensor_scalar(C.bias0[:], lens[:], key_col[:], -1e30, ALU.is_le, ALU.mult))
                ch(v.tensor_tensor(C.bias0[:], C.bias0[:], len0[:], ALU.mult))
                ch(v.tensor_scalar(len0[:], len0[:], -float(TK), float(TK), ALU.mult, ALU.add))
                ch(v.tensor_tensor(C.lens[:], lens[:], len0[:], ALU.max))
                dve.wait_ge(mask_in, 16)
                ch(v.tensor_reduce(lowest[:], mask_f[:], AX.X, ALU.min))
                ch(v.tensor_copy(C.lowest2[:], lowest[:]))
                ch(v.tensor_copy(C.mask2[:], mask_f[:]))
                ch(v.tensor_scalar(C.mask2_less[:], mask_f[:], lowest[:], None, ALU.subtract))
                dve.wait_ge(pack_in, 16)
                for l in range(4):
                    for w in (C.w(f"wq{l}"), C.w(f"bq{l}")):
                        ch(v.tensor_scalar(w, w, float(DH) ** -0.5, None, ALU.mult))
                for k, name in enumerate(("gate", "up", "down")):
                    m = C.w(name).rearrange("p (c d) -> p c d", c=3)
                    if name == "down":
                        ch(v.tensor_reduce(wabs[:, 6:7], C.w(name)[:, 0:I1], AX.X, ALU.max, apply_absolute_value=True))
                        for c in (7, 8):
                            ch(v.tensor_copy(wabs[:, c:c + 1], wabs[:, 6:7]))
                    else:
                        ch(v.tensor_reduce(wabs[:, 3 * k:3 * k + 3], m, AX.X, ALU.max, apply_absolute_value=True))
                ch(v.tensor_scalar(wscale[:], wabs[:], 1.0 / QMAX, None, ALU.mult))
                ch(v.tensor_copy(C.wscale[:], wscale[:]))
                ch(v.tensor_scalar(wscale[:], wscale[:], 1e-30, None, ALU.max))
                ch(v.reciprocal(winv[:], wscale[:]))
                for k, name in enumerate(("gate", "up", "down")):
                    m = C.w(name).rearrange("p (c d) -> p c d", c=3)
                    for c in range(3):
                        q = wint[:, 3 * k + c, :]
                        ch(v.tensor_scalar(q, m[:, c, :], winv[:, 3 * k + c:3 * k + c + 1], MAGIC, ALU.mult, ALU.add))
                        ch(v.tensor_scalar(q, q, MAGIC, -QMAX - 1.0, ALU.subtract, ALU.max))
                        ch(v.tensor_scalar(q, q, QMAX, None, ALU.min))
                ch(v.tensor_scalar(diag[:], C.ident[:], C.wscale[:, 6:7], None, ALU.mult))
                dve.sem_inc(quantized, 1)
                dve.wait_ge(rows_in, 16)
                for k, name in enumerate(("bf0", "bo2", "bp3")):
                    dve.wait_ge(folded_ready, k + 1)
                    r = C.row(name)
                    ch(v.tensor_tensor(r, C.bank[k][:, 0:D], r, ALU.add))
                for b in range(NB):
                    if b % (NB // nx) == 0:
                        dve.wait_ge(x_in, 16 * nx)
                    last = v.bn_stats(C.stats[:, b, :], C.x[:, b, :])
                ch(last)

            @block.tensor
            def _(pe):
                t = nc.tensor
                pe.wait_ge(made, 1)
                pe.wait_ge(pack_in, 16)
                for k, l in enumerate((0, 2, 3)):
                    t.matmul(C.bank[k][:, 0:D], C.w(f"bv{l}").to_broadcast([P, P]), C.w(f"wo{l}"),
                             start=True, stop=True).then_inc(folded_ready, 1)
                t.matmul(C.bank[3][:, 0:LEAVES], C.w("tree_q"), C.w("routers"), start=True, stop=True).then_inc(psum_ready, 1)
                for c in range(2):
                    o = PACK["leaves"][0] + P * c
                    t.matmul(C.bank[4 + c][:, 0:D], C.pack[:, o:o + P], C.w("tree_out"),
                             start=True, stop=True).then_inc(psum_ready, 1)
                pe.wait_ge(quantized, 1)
                for k in range(9):
                    if k >= 2:
                        pe.wait_ge(psum_read, 3 + k - 1)
                    t.transpose(C.bank[6 + k % 2][:, 0:P], wint[:, k, :], C.ident[:]).then_inc(psum_ready, 1)
                pe.wait_ge(psum_read, 3 + 8)
                t.matmul(C.bank[7][:, 128:256], ones[:], diag[:], start=True, stop=True).then_inc(psum_ready, 1)

            @block.scalar
            def _(act):
                for k in range(2):
                    s = slice(k * NB // 2, (k + 1) * NB // 2)
                    act.dma_start(C.ctxT[:, s, :], A["ctx"][:, s, :]).then_inc(ctx_in, 16)
                act.dma_start(C.w1[:], A["w1"]).then_inc(w_in, 16)
                a = nc.scalar
                act.wait_ge(psum_ready, 1)
                a.activation(C.route[:], C.bank[3][:, 0:LEAVES], ACT.Copy).then_inc(psum_read, 1)
                for c in range(2):
                    act.wait_ge(psum_ready, 2 + c)
                    a.activation(C.leaf[:, c, :], C.bank[4 + c][:, 0:D], ACT.Copy).then_inc(psum_read, 1)
                for k in range(9):
                    act.wait_ge(psum_ready, 4 + k)
                    a.activation(C.wquant[:, k, :], C.bank[6 + k % 2][:, 0:P], ACT.Copy).then_inc(psum_read, 1)
                act.wait_ge(psum_ready, 13)
                a.activation(C.down_scale[:], C.bank[7][:, 128:256], ACT.Copy).then_inc(psum_read, 1)
                act.wait_ge(ctx_in, 32)
                act.wait_ge(w_in, 16)
                act.wait_ge(psum_read, 13)



def attention(nc, C, l, bias_row):
    masked = {0: "lengths", 2: "mask"}.get(l)
    with Phase(nc, f"att{l}") as ph:
        xn = ph.sb("xn", [P, GB, D])
        xnT = ph.sb("xnT", [P, GT])
        q_full = ph.sb("q_full", [P, GT])
        k_full = ph.sb("k_full", [P, GK])
        q_part = ph.sb("q_part", [P, 2, GT], F16)
        k_part = ph.sb("k_part", [P, 2, GK], F16)
        q_stack = ph.sb("q_stack", [P, PART, GT], F16)
        q_block = [ph.sb(f"q_block{i}", [P, PART, PART, GT], F16) for i in range(2)]
        k_stack = [ph.sb(f"k_stack{i}", [P, PART, GK], F16) for i in range(2)]
        ctx = ph.sb("ctx", [P, GK])
        v_pad = [ph.sb(f"v_pad{i}", [P, GB, PART, PART, 32]) for i in range(2)]
        probs = [ph.sb(f"probs{i}", [P, PART, P]) for i in range(4)]
        top = ph.sb("top", [P, SLOTS, PART], BF16)
        inv_sum = ph.sb("inv_sum", [P, P])
        heads_out = [ph.sb(f"heads_out{i}", [P, P]) for i in range(2)]
        x_bias = [ph.sb(f"x_bias{i}", [P, GB, D]) for i in range(2)]
        S = C.bank[0:2]
        ST = C.bank[2:4]
        PV, SUM, OUT, PREP = C.bank[4:8]
        if masked == "lengths":
            mask0 = [ph.sb(f"mask0_{i}", [P, GB, TK], BF16) for i in range(2)]
        ns = norm_sems(ph)
        (xn_ready, xnT_psum, xnT_ready, q_psum, q_read, k_psum, k_read, v_psum, v_read, q_split, k_split, q_stacked,
         k_stacked, q_blocked, ctx_ready, scores, maxed, shifted, exps, weighed, inv_ready, normed, out_psum, added,
         xb_ready, padded, hi_ready, mask_ready, q_spilled, k_spilled) = (ph.sem(n) for n in (
             "xn_ready", "xnT_psum", "xnT_ready", "q_psum", "q_read", "k_psum", "k_read", "v_psum", "v_read", "q_split",
             "k_split", "q_stacked", "k_stacked", "q_blocked", "ctx_ready", "scores", "maxed", "shifted", "exps",
             "weighed", "inv_ready", "normed", "out_psum", "added", "xb_ready", "padded", "hi_ready", "mask_ready", "q_spilled", "k_spilled"))
        wk = C.w(f"wk{l}")
        NQ = PART * 16

        with nc.Block() as block:

            @block.tensor
            def _(pe):
                t = nc.tensor

                def form_scores(n, s, par):
                    b, j = s // PART, s % PART
                    wait(pe, maxed, 16 * n + s - 1)
                    if s == 0:
                        pe.wait_ge(q_blocked, PART * (n + 1))
                        pe.wait_ge(k_stacked, NQ * (n + 1))
                    o = S[s % 2][:, 0:GK].rearrange("p (g k) -> p g k", g=PART)
                    if masked == "lengths":
                        pe.wait_ge(mask_ready, n + 1)
                        m = mask0[par][:, b:b + 1, :].to_broadcast([P, PART, TK])
                        t.matmul(o, C.neg_big[:], m, start=True, stop=False)
                    if masked == "mask":
                        t.matmul(o, C.neg_big[:], C.mask2_less[:].unsqueeze(1).to_broadcast([P, PART, TK]),
                                 start=True, stop=False)
                    for g in range(PART):
                        last = t.matmul(o[:, g, :], q_block[par][:, j, g, b * P:(b + 1) * P],
                                        k_stack[par][:, j, b * TK:(b + 1) * TK],
                                        start=not masked, stop=not masked or g == PART - 1)
                    last.then_inc(scores, 1)

                def form_shifted(n, s, par):
                    b, j = s // PART, s % PART
                    wait(pe, exps, 16 * n + s - 1)
                    o = ST[s % 2][0:TK, :].rearrange("k (g q) -> k g q", g=PART)
                    t.matmul(o, k_stack[par][:, j, b * TK:(b + 1) * TK], q_block[par][:, j, :, b * P:(b + 1) * P],
                             start=True, stop=False)
                    if masked == "mask":
                        t.matmul(o, C.mask2[:], C.neg_big[:].unsqueeze(1).to_broadcast([P, PART, P]), start=False, stop=False)
                        t.matmul(o, C.lowest2[:].to_broadcast([P, TK]), C.pos_big[:].unsqueeze(1).to_broadcast([P, PART, P]),
                                 start=False, stop=False)
                    wait(pe, maxed, 16 * n + s + 1)
                    for g in range(PART):
                        last = t.matmul(o[:, g, :], top[:, s, g:g + 1].to_broadcast([P, TK]), C.neg_ident[:],
                                        start=False, stop=g == PART - 1)
                    last.then_inc(shifted, 1)

                def weigh(n, s, par):
                    b, j = s // PART, s % PART
                    pe.wait_ge(exps, 16 * n + s + 1)
                    if j == 0:
                        wait(pe, normed, 4 * n + b)
                        if b == 0:
                            pe.wait_ge(v_read, n + 1)
                    p = probs[s % 4]
                    for g in range(PART):
                        t.matmul(PV[32 * g:32 * g + 32, 0:P], v_pad[par][0:TK, b, g, j, :], p[0:TK, g, :],
                                 start=j == 0, stop=j == PART - 1)
                    for g in range(PART):
                        last = t.matmul(SUM[32 * g:32 * g + 32, 0:P], C.head_cols[0:TK, j, :], p[0:TK, g, :],
                                        start=j == 0, stop=j == PART - 1)
                    last.then_inc(weighed, 1)

                def project_out(n, b):
                    pe.wait_ge(normed, 4 * n + b + 1)
                    wait(pe, added, 4 * n + b)
                    if l == 1:
                        t.transpose(OUT[:, 0:D], heads_out[b % 2][:], C.ident[:]).then_inc(out_psum, 1)
                    else:
                        t.matmul(OUT[:, 0:D], heads_out[b % 2][:], C.w(f"wo{l}"), start=True, stop=True).then_inc(out_psum, 1)

                def prepare(n, step):
                    if step == 0:
                        pe.wait_ge(xn_ready, n + 1)
                        wait(pe, v_read, n)
                        for b in range(GB):
                            last = t.transpose(PREP[:, b * P:(b + 1) * P], xn[:, b, :], C.ident[:])
                        last.then_inc(xnT_psum, 1)
                    if step == 1:
                        pe.wait_ge(xnT_ready, n + 1)
                        t.matmul(PREP[:, :], C.w(f"wq{l}"), xnT[:], start=True, stop=True).then_inc(q_psum, 1)
                    if step == 2:
                        pe.wait_ge(q_read, n + 1)
                        pe.wait_ge(ctx_ready, n + 1)
                        t.matmul(PREP[:, 0:GK], wk, ctx[:], start=True, stop=True).then_inc(k_psum, 1)
                    if step == 3:
                        pe.wait_ge(k_read, n + 1)
                        for b in range(GB):
                            last = t.matmul(PREP[0:TK, b * D:(b + 1) * D], ctx[:, b * TK:(b + 1) * TK], C.w(f"wv{l}"),
                                            start=True, stop=True)
                        last.then_inc(v_psum, 1)

                for step in range(4):
                    prepare(0, step)
                for s in range(2):
                    form_scores(0, s, 0)

                def group(n, par, first, last_group):
                    for s in range(SLOTS):
                        form_shifted(n, s, par)
                        if s + 2 < SLOTS:
                            form_scores(n, s + 2, par)
                        elif not last_group:
                            form_scores(n + 1, s + 2 - SLOTS, 1 - par)
                        if s > 0:
                            weigh(n, s - 1, par)
                        elif not first:
                            weigh(n - 1, SLOTS - 1, 1 - par)
                        if s % PART == 1 and not (first and s == 1):
                            if s == 1:
                                project_out(n - 1, GB - 1)
                            else:
                                project_out(n, s // PART - 1)
                        if s % 2 == 0 and 2 <= s <= 8 and not last_group:
                            prepare(n + 1, s // 2 - 1)

                over_groups(pe, group)
                weigh(NG - 1, SLOTS - 1, (NG - 1) % 2)
                project_out(NG - 1, GB - 1)

            @block.scalar
            def _(act):
                a = nc.scalar

                def read_prepared(n, step, par):
                    if step == 0:
                        act.wait_ge(xnT_psum, n + 1)
                        wait(act, q_psum, n)
                        a.activation(xnT[:], PREP[:, :], ACT.Copy).then_inc(xnT_ready, 1)
                    if step == 1:
                        act.wait_ge(q_psum, n + 1)
                        wait(act, q_split, n)
                        a.activation(q_full[:], PREP[:, :], ACT.Identity, bias=C.w(f"bq{l}")).then_inc(q_read, 1)
                    if step == 2:
                        act.wait_ge(k_psum, n + 1)
                        wait(act, k_split, n)
                        a.activation(k_full[:], PREP[:, 0:GK], ACT.Identity, bias=C.w(f"bk{l}")).then_inc(k_read, 1)
                    if step == 3:
                        act.wait_ge(v_psum, n + 1)
                        wait(act, weighed, 16 * (n - 1))
                        if isinstance(n, int) and n < 2:
                            act.wait_ge(padded, 2)
                        for b in range(GB):
                            o = v_pad[par][0:TK, b, :, :, :].rearrange("k g j c -> k g (j c)")
                            o = diagonal(o)
                            last = a.activation(o, PREP[0:TK, b * D:(b + 1) * D].rearrange("k (g j d) -> k g j d", g=PART, j=PART),
                                                ACT.Copy)
                        last.then_inc(v_read, 1)

                def exponential(n, s):
                    act.wait_ge(shifted, 16 * n + s + 1)
                    wait(act, weighed, 16 * n + s - 3)
                    o, i = probs[s % 4][0:TK, :, :], ST[s % 2][0:TK, :].rearrange("k (g q) -> k g q", g=PART)
                    if masked == "lengths":
                        b = s // PART
                        apart(act, C)
                        last = a.activation(o, i, ACT.Exp, bias=C.bias0[0:TK, batch(n, b)], scale=C.keep0[0:TK, batch(n, b)])
                    else:
                        last = a.activation(o, i, ACT.Exp)
                    last.then_inc(exps, 1)

                for step in range(4):
                    read_prepared(0, step, 0)

                def group(n, par, first, last_group):
                    for s in range(SLOTS):
                        if s % 2 == 1 and 3 <= s <= 9 and not last_group:
                            read_prepared(n + 1, (s - 3) // 2, 1 - par)
                        exponential(n, s)

                over_groups(act, group)

            @block.vector
            def _(dve):
                v = nc.vector
                norm_vector(nc, C, dve, ns)

                def maximum(n, s):
                    dve.wait_ge(scores, 16 * n + s + 1)
                    wait(dve, shifted, 16 * n + s - 15)
                    v.tensor_reduce(top[:, s, :], S[s % 2][:, 0:GK].rearrange("p (g k) -> p g k", g=PART), AX.X, ALU.max)\
                        .then_inc(maxed, 1)

                def normalize(n, b):
                    dve.wait_ge(weighed, 16 * n + 4 * (b + 1))
                    v.reciprocal(inv_sum[:], SUM[:, 0:P]).then_inc(inv_ready, 1)
                    dve.wait_ge(inv_ready, 4 * n + b + 1)
                    wait(dve, out_psum, 4 * n + b - 1)
                    v.tensor_tensor(heads_out[b % 2][:], PV[:, 0:P], inv_sum[:], ALU.mult).then_inc(normed, 1)

                def add(n, b, par):
                    if b == 0:
                        dve.wait_ge(xb_ready, n + 1)
                    dve.wait_ge(out_psum, 4 * n + b + 1)
                    v.tensor_tensor(C.x[:, batch(n, b), :], OUT[:, 0:D].unsqueeze(1), x_bias[par][:, b:b + 1, :], ALU.add)\
                        .then_inc(added, 1)

                def statistics(n, b):
                    dve.wait_ge(added, 4 * n + b + 1)
                    return v.bn_stats(C.stats[:, batch(n, b), :], C.x[:, batch(n, b), :])

                def layer_norm(n):
                    wait(dve, xnT_psum, n)
                    normalized(nc, C, xn, n).then_inc(xn_ready, 1)

                def block_out(n, g, par):
                    if g == 0:
                        dve.wait_ge(q_stacked, NQ * (n + 1))
                        wait(dve, shifted, 16 * (n - 1))
                    v.tensor_scalar(q_block[par][:, :, g, :], q_stack[:], C.head_rows[:, g:g + 1], None, ALU.mult)\
                        .then_inc(q_blocked, 1)

                def key_masks(n, par):
                    wait(dve, scores, 16 * (n - 1))
                    apart(dve, C)
                    for b in range(GB):
                        last = v.tensor_scalar(mask0[par][:, b, :], C.key_row[:], C.lens[:, batch(n, b)], None, ALU.is_ge)
                    last.then_inc(mask_ready, 1)

                layer_norm(0)
                if masked == "lengths":
                    key_masks(0, 0)
                for g in range(PART):
                    block_out(0, g, 0)
                for s in range(2):
                    maximum(0, s)

                def group(n, par, first, last_group):
                    for s in range(SLOTS):
                        if s == 0 and not last_group:
                            layer_norm(n + 1)
                        if s == 6 and masked == "lengths" and not last_group:
                            key_masks(n + 1, 1 - par)
                        if s + 2 < SLOTS:
                            maximum(n, s + 2)
                        elif not last_group:
                            maximum(n + 1, s + 2 - SLOTS)
                        b = s // PART - 1
                        if s % PART == 0 and not (first and b < 0):
                            normalize(*((n - 1, GB - 1) if b < 0 else (n, b)))
                        if s % PART == 2 and not (first and b < 0):
                            add(*((n - 1, GB - 1, 1 - par) if b < 0 else (n, b, par)))
                        if s % PART == 3 and not (first and b < 0):
                            statistics(*((n - 1, GB - 1) if b < 0 else (n, b)))
                        if 9 <= s <= 12 and not last_group:
                            block_out(n + 1, s - 9, 1 - par)

                over_groups(dve, group)
                normalize(NG - 1, GB - 1)
                add(NG - 1, GB - 1, (NG - 1) % 2)
                statistics(NG - 1, GB - 1)

            @block.gpsimd
            def _(pool):
                g = nc.gpsimd
                for i in range(2):
                    g.memset(v_pad[i][:], 0.0).then_inc(padded, 1)
                norm_pool(nc, C, pool, ns)

                def split(n, full, part, ready, was_stacked, done, width):
                    pool.wait_ge(ready, n + 1)
                    wait(pool, was_stacked, NQ * n)
                    apart(pool, C)
                    g.tensor_copy(part[:, 0, :], full[:]).then_inc(hi_ready, 1)
                    pool.wait_ge(hi_ready, 2 * n + (1 if done is q_split else 2))
                    g.tensor_tensor(part[:, 1, :], full[:], part[:, 0, :], ALU.subtract).then_inc(done, 1)

                def group(n, par, first, last_group):
                    wait(pool, v_psum, n)
                    apart(pool, C)
                    g.tensor_copy(ctx[:].rearrange("p (b k) -> p b k", b=GB), C.ctxT[:, batch(n, 0, GB), :]).then_inc(ctx_ready, 1)
                    split(n, q_full, q_part, q_read, q_stacked, q_split, GT)
                    split(n, k_full, k_part, k_read, k_stacked, k_split, GK)
                    wait(pool, added, 4 * (n - 1))
                    g.tensor_tensor(x_bias[par][:], C.x[:, batch(n, 0, GB), :],
                                    bias_row.unsqueeze(1).to_broadcast([P, GB, D]), ALU.add).then_inc(xb_ready, 1)

                over_groups(pool, group)

            @block.sync
            def _(sp):
                def restack(n, part, split_done, scratch, spilled, stack, stacked, halves, free):
                    sp.wait_ge(split_done, n + 1)
                    apart(sp, C)
                    sp.dma_start(scratch[:, :, :].rearrange("h f t -> f h t"), part[:]).then_inc(spilled, 16)
                    sp.wait_ge(spilled, 16 * (n + 1))
                    apart(sp, C)
                    wait(sp, *free)
                    apart(sp, C)
                    for p in range(PART):
                        sp.dma_start(stack[32 * p:32 * p + 32, :, :], scratch[halves[p], :, :].rearrange("(j r) t -> r j t", j=PART))\
                            .then_inc(stacked, 16)

                def group(n, par, first, last_group):
                    restack(n, q_part, q_split, C.q_scratch, q_spilled, q_stack, q_stacked, (0, 0, 1, 1), (q_blocked, PART * n))
                    restack(n, k_part, k_split, C.k_scratch, k_spilled, k_stack[par], k_stacked, (0, 1, 0, 1),
                            (shifted, 16 * (n - 1)))

                over_groups(sp, group)



def experts(nc, C, A):
    with Phase(nc, "moe") as ph:
        w2 = ph.sb("w2", [P, E, FC, D])
        xn = ph.sb("xn", [P, GB, D])
        xnT = [ph.sb(f"xnT{i}", [P, GT]) for i in range(2)]
        hid = [ph.sb(f"hid{i}", [P, FC, GT]) for i in range(2)]
        most = ph.sb("most", [P, GB])
        prob = ph.sb("prob", [P, GB, E])
        total = ph.sb("total", [P, GB])
        above = ph.sb("above", [P, GB, E, E])
        rank = ph.sb("rank", [P, GB, E])
        weight = [ph.sb(f"weight{i}", [P, GB, E]) for i in range(2)]
        H, Y, PREP, LOGITS = C.bank[0:4], C.bank[4:6], C.bank[6], C.bank[7]
        ns = norm_sems(ph)
        (w2_in, xn_ready, xnT_psum, xnT_ready, logits_ready, less_most, exps, weights_ready, hidden, silus, y_ready, added,
         route_step, zeroed) = (ph.sem(n) for n in (
             "w2_in", "xn_ready", "xnT_psum", "xnT_ready", "logits_ready", "less_most", "exps", "weights_ready", "hidden",
             "silus", "y_ready", "added", "route_step", "zeroed"))
        STEPS = 2 * E + 3

        with nc.Block() as block:

            @block.sync
            def _(sp):
                for e in range(E):
                    sp.dma_start(w2[:, e, :, :], A["w2"][:, e, :, :]).then_inc(w2_in, 16)

            @block.tensor
            def _(pe):
                t = nc.tensor

                def prepare(n, step, par):
                    if step == 0:
                        pe.wait_ge(xn_ready, n + 1)
                        wait(pe, xnT_ready, n)
                        for b in range(GB):
                            last = t.transpose(PREP[:, b * P:(b + 1) * P], xn[:, b, :], C.ident[:])
                        last.then_inc(xnT_psum, 1)
                    else:
                        pe.wait_ge(xnT_ready, n + 1)
                        wait(pe, less_most, n)
                        for b in range(GB):
                            last = t.matmul(LOGITS[:, b * E:(b + 1) * E], xnT[par][:, b * P:(b + 1) * P], C.w("choice"),
                                            start=True, stop=True)
                        last.then_inc(logits_ready, 1)

                def first(n, e, c, par):
                    q = n * E + e
                    if e == 0 and c == 0:
                        pe.wait_ge(xnT_ready, n + 1)
                    wait(pe, silus, 4 * (q - 1) + c + 1)
                    t.matmul(H[c][:, :], C.w1[:, e, c, :], xnT[par][:], start=True, stop=True).then_inc(hidden, 1)

                def second(n, e, b):
                    q = n * E + e
                    if b == 0:
                        pe.wait_ge(silus, 4 * q + 4)
                        wait(pe, added, q - 1)
                    for c in range(FC):
                        last = t.matmul(Y[e % 2][:, b * D:(b + 1) * D], hid[e % 2][:, c, b * P:(b + 1) * P], w2[:, e, c, :],
                                        start=c == 0, stop=c == FC - 1)
                    if b == GB - 1:
                        last.then_inc(y_ready, 1)

                prepare(0, 0, 0)
                prepare(0, 1, 0)
                for c in range(FC):
                    first(0, 0, c, 0)

                def group(n, par, is_first, is_last):
                    for e in range(E):
                        if is_first:
                            pe.wait_ge(w2_in, 16 * E)
                        for c in range(FC):
                            if e + 1 < E:
                                first(n, e + 1, c, par)
                            elif not is_last:
                                first(n + 1, 0, c, 1 - par)
                            if e < 2 and c == 1 and not is_last:
                                prepare(n + 1, e, 1 - par)
                            second(n, e, c)

                over_groups(pe, group)

            @block.scalar
            def _(act):
                a = nc.scalar

                def transposed(n, par):
                    act.wait_ge(xnT_psum, n + 1)
                    wait(act, hidden, 32 * (n - 1))
                    a.activation(xnT[par][:], PREP[:, :], ACT.Copy).then_inc(xnT_ready, 1)

                def exponential(n):
                    act.wait_ge(less_most, n + 1)
                    a.activation(prob[:], prob[:], ACT.Exp).then_inc(exps, 1)

                def silu(n, e, c):
                    q = n * E + e
                    act.wait_ge(hidden, 4 * q + c + 1)
                    if c == 0:
                        wait(act, y_ready, q - 1)
                    a.activation(hid[e % 2][:, c, :], H[c][:, :], ACT.Silu).then_inc(silus, 1)

                transposed(0, 0)
                exponential(0)
                for c in range(FC):
                    silu(0, 0, c)

                def group(n, par, is_first, is_last):
                    for e in range(E):
                        for c in range(FC):
                            if e + 1 < E:
                                silu(n, e + 1, c)
                            elif not is_last:
                                silu(n + 1, 0, c)
                            if e == 0 and c == 1 and not is_last:
                                transposed(n + 1, 1 - par)
                        if e == 2 and not is_last:
                            exponential(n + 1)

                over_groups(act, group)

            @block.vector
            def _(dve):
                v = nc.vector
                norm_vector(nc, C, dve, ns)

                def layer_norm(n):
                    wait(dve, xnT_psum, n)
                    normalized(nc, C, xn, n).then_inc(xn_ready, 1)

                def less_maximum(n):
                    dve.wait_ge(logits_ready, n + 1)
                    wait(dve, route_step, STEPS * n)
                    lg = LOGITS[:, 0:GB * E].rearrange("p (b e) -> p b e", b=GB)
                    v.tensor_reduce(most[:], lg, AX.X, ALU.max).then_inc(route_step, 1)
                    dve.wait_ge(route_step, STEPS * n + 1)
                    v.tensor_tensor(prob[:], lg, most[:].unsqueeze(2).to_broadcast([P, GB, E]), ALU.subtract)\
                        .then_inc(less_most, 1)

                def route(n, par):
                    base = STEPS * n + 1
                    dve.wait_ge(exps, n + 1)
                    v.tensor_reduce(total[:], prob[:], AX.X, ALU.add).then_inc(route_step, 1)
                    dve.wait_ge(route_step, base + 1)
                    v.reciprocal(total[:], total[:]).then_inc(route_step, 1)
                    dve.wait_ge(route_step, base + 2)
                    v.tensor_tensor(prob[:], prob[:], total[:].unsqueeze(2).to_broadcast([P, GB, E]), ALU.mult)\
                        .then_inc(route_step, 1)
                    dve.wait_ge(route_step, base + 3)
                    for e in range(E):
                        if e + 1 < E:
                            v.tensor_tensor(above[:, :, e, e + 1:], prob[:, :, e:e + 1].to_broadcast([P, GB, E - 1 - e]),
                                            prob[:, :, e + 1:], ALU.is_ge).then_inc(route_step, 1)
                        if e:
                            v.tensor_tensor(above[:, :, e, 0:e], prob[:, :, e:e + 1].to_broadcast([P, GB, e]),
                                            prob[:, :, 0:e], ALU.is_gt).then_inc(route_step, 1)
                    dve.wait_ge(route_step, base + 3 + 2 * E - 2)
                    v.tensor_reduce(rank[:], above[:].rearrange("p b f e -> p b e f"), AX.X, ALU.add).then_inc(route_step, 1)
                    dve.wait_ge(route_step, base + 2 + 2 * E)
                    v.scalar_tensor_tensor(out=weight[par][:], in0=rank[:], scalar=1.5, in1=prob[:], op0=ALU.is_lt, op1=ALU.mult)\
                        .then_inc(weights_ready, 1)

                def add(n, e, par):
                    q = n * E + e
                    dve.wait_ge(y_ready, q + 1)
                    if e == 0:
                        dve.wait_ge(weights_ready, n + 1)
                    else:
                        dve.wait_ge(added, q)
                    for b in range(GB):
                        xb = C.x[:, batch(n, b), :]
                        last = v.scalar_tensor_tensor(out=xb, in0=Y[e % 2][:, b * D:(b + 1) * D].unsqueeze(1),
                                                      scalar=weight[par][:, b, e:e + 1], in1=xb, op0=ALU.mult, op1=ALU.add)
                    last.then_inc(added, 1)

                layer_norm(0)
                v.memset(above[:], 0.0).then_inc(zeroed, 1)
                dve.wait_ge(zeroed, 1)
                less_maximum(0)
                route(0, 0)

                def group(n, par, is_first, is_last):
                    if not is_last:
                        layer_norm(n + 1)
                    for e in range(E):
                        add(n, e, par)
                        if e == 2 and not is_last:
                            less_maximum(n + 1)
                        if e == 3 and not is_last:
                            route(n + 1, 1 - par)
                    dve.wait_ge(added, n * E + E)
                    for b in range(GB):
                        v.bn_stats(C.stats[:, batch(n, b), :], C.x[:, batch(n, b), :])

                over_groups(dve, group)
                v.engine_nop().then_inc(zeroed, 1)
                dve.wait_ge(zeroed, 2)

            @block.gpsimd
            def _(pool):
                norm_pool(nc, C, pool, ns)



def quantized_gated(nc, C):
    with nc.sbuf_tensor("gated", [P, 3, NB * P], F32) as h:
        with Phase(nc, "qmax") as ph:
            xn = [ph.sb(f"xn{i}", [P, GB, D]) for i in range(2)]
            peaks = ph.sb("peaks", [P, NG])
            ns = norm_sems(ph)
            xn_ready, peak_read, step, peak_ready, peak_all, clip_ready = (
                ph.sem(n) for n in ("xn_ready", "peak_read", "step", "peak_ready", "peak_all", "clip_ready"))
            with nc.Block() as block:

                @block.vector
                def _(dve):
                    v = nc.vector
                    norm_vector(nc, C, dve, ns)

                    def group(n, par, first, last):
                        normalized(nc, C, xn[par], n).then_inc(xn_ready, 1)
                        dve.wait_ge(xn_ready, n + 1)
                        v.tensor_reduce(peaks[:, bass.ds(n, 1)], xn[par][:], AX.XY, ALU.max, apply_absolute_value=True)\
                            .then_inc(peak_read, 1)

                    over_groups(dve, group)
                    dve.wait_ge(peak_read, NG)
                    v.tensor_reduce(C.peak[:, 0:1], peaks[:], AX.X, ALU.max).then_inc(peak_ready, 1)
                    dve.wait_ge(peak_all, 1)
                    dve.wait_ge(clip_ready, 1)
                    activation_scale(nc, C, dve, step, 0)

                @block.gpsimd
                def _(pool):
                    norm_pool(nc, C, pool, ns)
                    all_peak(nc, C, pool, peak_ready, peak_all, 0)

                @block.scalar
                def _(act):
                    c = ROWS["clip_x"][0]
                    nc.scalar.activation(C.clip[:], C.rows[:, c:c + 2], ACT.Sigmoid).then_inc(clip_ready, 1)

        with Phase(nc, "qup") as ph:
            xn = [ph.sb(f"xn{i}", [P, GB, D]) for i in range(2)]
            xi = [ph.sb(f"xi{i}", [P, GB, D]) for i in range(2)]
            xqT = [ph.sb(f"xqT{i}", [P, GT], BF16) for i in range(2)]
            gate = ph.sb("gate", [P, 3, GT])
            scales = ph.sb("scales", [P, 6])
            peaks = ph.sb("peaks", [P, NG])
            unmagic = ph.sb("unmagic", [P, 1])
            (xn_ready, rounded, xi_ready, xT_psum, xq_ready, gates, ups, silus, h_ready, peak_read, step, peak_ready,
             peak_all, scales_ready, const_ready) = (ph.sem(n) for n in (
                 "xn_ready", "rounded", "xi_ready", "xT_psum", "xq_ready", "gates", "ups", "silus", "h_ready", "peak_read",
                 "step", "peak_ready", "peak_all", "scales_ready", "const_ready"))
            G, U, PREP = C.bank[0:3], C.bank[3:6], C.bank[6:8]
            with nc.Block() as block:

                @block.vector
                def _(dve):
                    v = nc.vector
                    v.tensor_scalar(scales[:], C.wscale[:, 0:6], C.scale[:, 0:1], None, ALU.mult).then_inc(scales_ready, 1)
                    dve.wait_ge(scales_ready, 1)

                    def layer_norm(n, par):
                        wait(dve, rounded, n - 1)
                        normalized(nc, C, xn[par], n).then_inc(xn_ready, 1)

                    layer_norm(0, 0)

                    def group(n, par, first, last_group):
                        if not last_group:
                            layer_norm(n + 1, 1 - par)
                        for c in range(3):
                            dve.wait_ge(silus, 3 * n + c + 1)
                            dve.wait_ge(ups, 3 * n + c + 1)
                            v.scalar_tensor_tensor(out=h[:, c, bass.ds(n * GT, GT)], in0=U[c][:, :], scalar=scales[:, 3 + c:4 + c],
                                                   in1=gate[:, c, :], op0=ALU.mult, op1=ALU.mult).then_inc(h_ready, 1)
                        dve.wait_ge(h_ready, 3 * n + 3)
                        v.tensor_reduce(peaks[:, bass.ds(n, 1)], h[:, :, bass.ds(n * GT, GT)], AX.XY, ALU.max,
                                        apply_absolute_value=True).then_inc(peak_read, 1)

                    over_groups(dve, group)
                    dve.wait_ge(peak_read, NG)
                    v.tensor_reduce(C.peak[:, 1:2], peaks[:], AX.X, ALU.max).then_inc(peak_ready, 1)
                    dve.wait_ge(peak_all, 1)
                    activation_scale(nc, C, dve, step, 1)

                @block.gpsimd
                def _(pool):
                    g = nc.gpsimd
                    g.memset(unmagic[:], -MAGIC).then_inc(const_ready, 1)

                    def group(n, par, first, last_group):
                        round_clipped(C, pool, xi[par][:], xn[par][:], C.scale[:, 2:3], xn_ready, n, (xT_psum, n - 1), rounded,
                                      xi_ready, g)

                    over_groups(pool, group)
                    all_peak(nc, C, pool, peak_ready, peak_all, 1)

                @block.scalar
                def _(act):
                    a = nc.scalar
                    act.wait_ge(const_ready, 1)

                    def integers(n, par):
                        act.wait_ge(xT_psum, n + 1)
                        wait(act, ups, 3 * (n - 1))
                        a.activation(xqT[par][:], PREP[par][:, :], ACT.Identity, bias=unmagic[:]).then_inc(xq_ready, 1)

                    integers(0, 0)
                    act.wait_ge(scales_ready, 1)

                    def group(n, par, first, last_group):
                        if not last_group:
                            integers(n + 1, 1 - par)
                        for c in range(3):
                            act.wait_ge(gates, 3 * n + c + 1)
                            wait(act, h_ready, 3 * (n - 1) + c + 1)
                            a.activation(gate[:, c, :], G[c][:, :], ACT.Silu, scale=scales[:, c:c + 1]).then_inc(silus, 1)

                    over_groups(act, group)

                @block.tensor
                def _(pe):
                    t = nc.tensor

                    def turn(n, par):
                        pe.wait_ge(xi_ready, n + 1)
                        wait(pe, xq_ready, n - 1)
                        for b in range(GB):
                            last = t.transpose(PREP[par][:, b * P:(b + 1) * P], xi[par][:, b, :], C.ident[:])
                        last.then_inc(xT_psum, 1)

                    turn(0, 0)

                    def group(n, par, first, last_group):
                        if not last_group:
                            turn(n + 1, 1 - par)
                        pe.wait_ge(xq_ready, n + 1)
                        for c in range(3):
                            wait(pe, silus, 3 * (n - 1) + c + 1)
                            t.matmul(G[c][:, :], C.wquant[:, c, :], xqT[par][:], start=True, stop=True).then_inc(gates, 1)
                            wait(pe, h_ready, 3 * (n - 1) + c + 1)
                            t.matmul(U[c][:, :], C.wquant[:, 3 + c, :], xqT[par][:], start=True, stop=True).then_inc(ups, 1)

                    over_groups(pe, group)

        with Phase(nc, "qdown") as ph:
            hq = [ph.sb(f"hq{i}", [P, 3, GT], BF16) for i in range(2)]
            out = ph.sb("out", [P, GB, D])
            col_scale = ph.sb("col_scale", [P, D])
            unmagic = ph.sb("unmagic", [P, 1])
            (rounded, hi_ready, hq_ready, downs, scaled, added, col_ready, const_ready) = (ph.sem(n) for n in (
                "rounded", "hi_ready", "hq_ready", "downs", "scaled", "added", "col_ready", "const_ready"))
            Y = C.bank[0:2]
            with nc.Block() as block:

                @block.gpsimd
                def _(pool):
                    nc.gpsimd.memset(unmagic[:], -MAGIC).then_inc(const_ready, 1)

                @block.scalar
                def _(act):
                    act.wait_ge(const_ready, 1)

                    def group(n, par, first, last_group):
                        act.wait_ge(hi_ready, n + 1)
                        wait(act, downs, n - 1)
                        nc.scalar.activation(hq[par][:], h[:, :, bass.ds(n * GT, GT)], ACT.Identity, bias=unmagic[:]).then_inc(hq_ready, 1)

                    over_groups(act, group)

                @block.tensor
                def _(pe):
                    def group(n, par, first, last_group):
                        pe.wait_ge(hq_ready, n + 1)
                        wait(pe, scaled, n - 1)
                        for b in range(GB):
                            for c in range(3):
                                last = nc.tensor.matmul(Y[par][:, b * D:(b + 1) * D], hq[par][:, c, b * P:(b + 1) * P],
                                                        C.wquant[:, 6 + c, :], start=c == 0, stop=c == 2)
                        last.then_inc(downs, 1)

                    over_groups(pe, group)

                @block.vector
                def _(dve):
                    v = nc.vector
                    v.tensor_scalar(col_scale[:], C.down_scale[:], C.scale[:, 1:2], None, ALU.mult).then_inc(col_ready, 1)
                    dve.wait_ge(col_ready, 1)

                    def integers(n):
                        part = h[:, :, bass.ds(n * GT, GT)]
                        v.tensor_scalar(part, part, C.scale[:, 3:4], MAGIC, ALU.mult, ALU.add).then_inc(rounded, 1)
                        dve.wait_ge(rounded, n + 1)
                        v.tensor_scalar(part, part, MAGIC + QMAX, MAGIC - QMAX - 1.0, ALU.min, ALU.max).then_inc(hi_ready, 1)

                    integers(0)

                    def group(n, par, first, last_group):
                        if not last_group:
                            integers(n + 1)
                        dve.wait_ge(downs, n + 1)
                        v.tensor_tensor(out[:], Y[par][:, :].rearrange("p (b d) -> p b d", b=GB),
                                        col_scale[:].unsqueeze(1).to_broadcast([P, GB, D]), ALU.mult).then_inc(scaled, 1)
                        dve.wait_ge(scaled, n + 1)
                        xg = C.x[:, batch(n, 0, GB), :]
                        v.tensor_tensor(xg, xg, out[:], ALU.add).then_inc(added, 1)
                        dve.wait_ge(added, n + 1)
                        for b in range(GB):
                            last = v.bn_stats(C.stats[:, batch(n, b), :], C.x[:, batch(n, b), :])

                    over_groups(dve, group)
                    v.engine_nop().then_inc(col_ready, 1)
                    dve.wait_ge(col_ready, 2)


def activation_scale(nc, C, dve, step, k):
    ch = Chain(dve, step)
    ch(nc.vector.tensor_scalar(C.scale[:, k:k + 1], C.peak[:, 2 + k:3 + k], C.clip[:, k:k + 1], 1.0 / QMAX, ALU.mult, ALU.mult))
    ch(nc.vector.reciprocal(C.scale[:, 2 + k:3 + k], C.scale[:, k:k + 1]))


def all_peak(nc, C, pool, ready, done, k):
    pool.wait_ge(ready, 1)
    nc.gpsimd.partition_all_reduce(C.peak[:, 2 + k:3 + k], C.peak[:, k:k + 1], P, bass.bass_isa.ReduceOp.max).then_inc(done, 1)


def round_clipped(C, pool, out, x, inv, ready, n, free, rounded, done, g):
    if ready is not None:
        pool.wait_ge(ready, n + 1)
    wait(pool, *free)
    apart(pool, C)
    g.tensor_scalar(out, x, inv, MAGIC, ALU.mult, ALU.add).then_inc(rounded, 1)
    pool.wait_ge(rounded, n + 1)
    apart(pool, C)
    g.tensor_scalar(out, out, MAGIC + QMAX, MAGIC - QMAX - 1.0, ALU.min, ALU.max).then_inc(done, 1)



def tree(nc, C):
    with Phase(nc, "tree") as ph:
        xn = ph.sb("xn", [P, GB, D])
        xnT = [ph.sb(f"xnT{i}", [P, GT]) for i in range(2)]
        right = [ph.sb(f"right{i}", [P, GB, LEAVES]) for i in range(2)]
        left = ph.sb("left", [P, GB, LEAVES])
        level = [ph.sb(f"level{i}", [P, GB, LEAVES // 2]) for i in range(2)]
        leaf = [ph.sb(f"leaf{i}", [P, GB, LEAVES]) for i in range(2)]
        leafT = ph.sb("leafT", [P, 2, GT])
        x_bias = [ph.sb(f"x_bias{i}", [P, GB, D]) for i in range(2)]
        PREP, G, LT, OUT = C.bank[0], C.bank[1:3], C.bank[3:5], C.bank[5:7]
        ns = norm_sems(ph)
        (xn_ready, xnT_psum, xnT_ready, gates, rights, step, leaves, leafT_psum, leafT_ready, outs, added, xb_ready, end) = (
            ph.sem(n) for n in ("xn_ready", "xnT_psum", "xnT_ready", "gates", "rights", "step", "leaves", "leafT_psum",
                                "leafT_ready", "outs", "added", "xb_ready", "end"))
        DEPTH = 8
        STEPS = 1 + 2 * (DEPTH - 1)
        with nc.Block() as block:

            @block.tensor
            def _(pe):
                t = nc.tensor

                def turn(n, par):
                    pe.wait_ge(xn_ready, n + 1)
                    wait(pe, xnT_ready, n)
                    for b in range(GB):
                        last = t.transpose(PREP[:, b * P:(b + 1) * P], xn[:, b, :], C.ident[:])
                    last.then_inc(xnT_psum, 1)

                def route(n, par):
                    pe.wait_ge(xnT_ready, n + 1)
                    for k in range(2):
                        wait(pe, rights, 2 * (n - 1) + k + 1)
                        for b in range(2):
                            last = t.matmul(G[k][:, b * LEAVES:(b + 1) * LEAVES], xnT[par][:, (2 * k + b) * P:(2 * k + b + 1) * P],
                                            C.route[:], start=True, stop=True)
                        last.then_inc(gates, 1)

                turn(0, 0)
                route(0, 0)

                def group(n, par, first, last_group):
                    if not last_group:
                        turn(n + 1, 1 - par)
                        route(n + 1, 1 - par)
                    pe.wait_ge(leaves, n + 1)
                    for c in range(2):
                        wait(pe, leafT_ready, 2 * (n - 1) + c + 1)
                        for b in range(GB):
                            last = t.transpose(LT[c][:, b * P:(b + 1) * P], leaf[par][:, b, c * P:(c + 1) * P], C.ident[:])
                        last.then_inc(leafT_psum, 1)
                    pe.wait_ge(leafT_ready, 2 * n + 2)
                    wait(pe, added, n - 1)
                    for b in range(GB):
                        for c in range(2):
                            last = t.matmul(OUT[par][:, b * D:(b + 1) * D], leafT[:, c, b * P:(b + 1) * P], C.leaf[:, c, :],
                                            start=c == 0, stop=c == 1)
                    last.then_inc(outs, 1)

                over_groups(pe, group)

            @block.scalar
            def _(act):
                a = nc.scalar

                def transposed(n, par):
                    act.wait_ge(xnT_psum, n + 1)
                    wait(act, gates, 2 * (n - 1))
                    a.activation(xnT[par][:], PREP[:, :], ACT.Copy).then_inc(xnT_ready, 1)

                def sigmoids(n, par):
                    wait(act, leaves, n - 1)
                    for k in range(2):
                        act.wait_ge(gates, 2 * n + k + 1)
                        a.activation(right[par][:, 2 * k:2 * k + 2, :], G[k][:, :].rearrange("p (b m) -> p b m", b=2), ACT.Sigmoid)\
                            .then_inc(rights, 1)

                transposed(0, 0)
                sigmoids(0, 0)

                def group(n, par, first, last_group):
                    if not last_group:
                        transposed(n + 1, 1 - par)
                        sigmoids(n + 1, 1 - par)
                    wait(act, outs, n)
                    for c in range(2):
                        act.wait_ge(leafT_psum, 2 * n + c + 1)
                        a.activation(leafT[:, c, :], LT[c][:, :], ACT.Copy).then_inc(leafT_ready, 1)

                over_groups(act, group)

            @block.vector
            def _(dve):
                v = nc.vector
                norm_vector(nc, C, dve, ns)

                def layer_norm(n):
                    wait(dve, xnT_psum, n)
                    normalized(nc, C, xn, n).then_inc(xn_ready, 1)

                def add(n, par):
                    dve.wait_ge(outs, n + 1)
                    dve.wait_ge(xb_ready, n + 1)
                    v.tensor_tensor(C.x[:, batch(n, 0, GB), :], OUT[par][:, :].rearrange("p (b d) -> p b d", b=GB),
                                    x_bias[par][:], ALU.add).then_inc(added, 1)
                    dve.wait_ge(added, n + 1)
                    for b in range(GB):
                        v.bn_stats(C.stats[:, batch(n, b), :], C.x[:, batch(n, b), :])

                def descend(n, par):
                    dve.wait_ge(rights, 2 * n + 2)
                    base = STEPS * n
                    wait(dve, step, base)
                    wait(dve, leaves, n)
                    r = right[par]
                    v.tensor_scalar(left[:], r[:], -1.0, 1.0, ALU.mult, ALU.add).then_inc(step, 1)
                    dve.wait_ge(step, base + 1)
                    v.tensor_copy(level[0][:, :, 0:1], left[:, :, 0:1]).then_inc(step, 1)
                    v.tensor_copy(level[0][:, :, 1:2], r[:, :, 0:1]).then_inc(step, 1)
                    for k in range(1, DEPTH):
                        nodes = 2 ** k
                        dve.wait_ge(step, base + 1 + 2 * k)
                        if k == DEPTH - 1:
                            wait(dve, leafT_psum, 2 * (n - 1))
                        o = leaf[par] if k == DEPTH - 1 else level[k % 2]
                        o = o[:, :, 0:2 * nodes].rearrange("p b (m s) -> p b m s", s=2)
                        i = level[(k - 1) % 2][:, :, 0:nodes]
                        first_child = v.tensor_tensor(o[:, :, :, 0], i, left[:, :, nodes - 1:2 * nodes - 1], ALU.mult)
                        second_child = v.tensor_tensor(o[:, :, :, 1], i, r[:, :, nodes - 1:2 * nodes - 1], ALU.mult)
                        if k == DEPTH - 1:
                            second_child.then_inc(leaves, 1)
                        else:
                            first_child.then_inc(step, 1)
                            second_child.then_inc(step, 1)

                layer_norm(0)

                def group(n, par, first, last_group):
                    if not last_group:
                        layer_norm(n + 1)
                    descend(n, par)
                    if not first:
                        add(n - 1, 1 - par)

                over_groups(dve, group)
                add(NG - 1, (NG - 1) % 2)
                v.engine_nop().then_inc(end, 1)
                dve.wait_ge(end, 1)

            @block.gpsimd
            def _(pool):
                norm_pool(nc, C, pool, ns)
                biased(nc, C, pool, x_bias, C.row("tree_b"), added, xb_ready)


def biased(nc, C, pool, x_bias, bias_row, added, xb_ready):
    def group(n, par, first, last_group):
        wait(pool, added, n - 1)
        nc.gpsimd.tensor_tensor(x_bias[par][:], C.x[:, batch(n, 0, GB), :], bias_row.unsqueeze(1).to_broadcast([P, GB, D]),
                                ALU.add).then_inc(xb_ready, 1)

    over_groups(pool, group)



def channel_mix(nc, C, A):
    with Phase(nc, "mix") as ph:
        xn = ph.sb("xn", [P, GB, D])
        xT = [ph.sb(f"xT{i}", [P, GB, P + 1]) for i in range(2)]
        step_back = ph.sb("step_back", [P, GB, P])
        xr = [ph.sb(f"xr{i}", [P, GB, P]) for i in range(2)]
        xk = [ph.sb(f"xk{i}", [P, GB, P]) for i in range(2)]
        relu = ph.sb("relu", [P, GT])
        kact = ph.sb("kact", [P, GT])
        gate = [ph.sb(f"gate{i}", [P, GB, D]) for i in range(2)]
        out = [ph.sb(f"out{i}", [P, GB, D]) for i in range(2)]
        PREP, R, K, V = C.bank[0], C.bank[1:3], C.bank[3:5], C.bank[5:7]
        ns = norm_sems(ph)
        (zeroed, xn_ready, xT_psum, xT_ready, back_ready, mixed, r_psum, k_psum, v_psum, relus, squares, gates, products,
         finals, stored) = (ph.sem(n) for n in (
             "zeroed", "xn_ready", "xT_psum", "xT_ready", "back_ready", "mixed", "r_psum", "k_psum", "v_psum", "relus",
             "squares", "gates", "products", "finals", "stored"))
        with nc.Block() as block:

            @block.tensor
            def _(pe):
                t = nc.tensor

                def turn(n):
                    pe.wait_ge(xn_ready, n + 1)
                    wait(pe, xT_ready, n)
                    for b in range(GB):
                        last = t.transpose(PREP[:, b * P:(b + 1) * P], xn[:, b, :], C.ident[:])
                    last.then_inc(xT_psum, 1)

                turn(0)

                def group(n, par, first, last_group):
                    if not last_group:
                        turn(n + 1)
                    pe.wait_ge(mixed, 2 * n + 2)
                    wait(pe, relus, n - 1)
                    t.matmul(K[par][:, :], C.w("mix_k"), xk[par][:].rearrange("p b t -> p (b t)"), start=True, stop=True)\
                        .then_inc(k_psum, 1)
                    wait(pe, gates, n - 1)
                    for b in range(GB):
                        last = t.matmul(R[par][:, b * D:(b + 1) * D], xr[par][:, b, :], C.w("mix_r"), start=True, stop=True)
                    last.then_inc(r_psum, 1)
                    pe.wait_ge(squares, n + 1)
                    wait(pe, products, n - 1)
                    for b in range(GB):
                        last = t.matmul(V[par][:, b * D:(b + 1) * D], kact[:, b * P:(b + 1) * P], C.w("mix_v"), start=True, stop=True)
                    last.then_inc(v_psum, 1)

                over_groups(pe, group)

            @block.scalar
            def _(act):
                a = nc.scalar
                act.wait_ge(zeroed, 2)

                def transposed(n, par):
                    act.wait_ge(xT_psum, n + 1)
                    wait(act, mixed, 2 * (n - 1))
                    a.activation(xT[par][:, :, 1:], PREP[:, :].rearrange("p (b t) -> p b t", b=GB), ACT.Copy).then_inc(xT_ready, 1)

                transposed(0, 0)

                def group(n, par, first, last_group):
                    if not last_group:
                        transposed(n + 1, 1 - par)
                    act.wait_ge(k_psum, n + 1)
                    wait(act, squares, n)
                    a.activation(relu[:], K[par][:, :], ACT.Relu).then_inc(relus, 1)
                    act.wait_ge(r_psum, n + 1)
                    wait(act, products, n - 1)
                    a.activation(gate[par][:], R[par][:, :].rearrange("p (b d) -> p b d", b=GB), ACT.Sigmoid).then_inc(gates, 1)

                over_groups(act, group)

            @block.vector
            def _(dve):
                v = nc.vector
                for i in range(2):
                    v.memset(xT[i][:, :, 0:1], 0.0).then_inc(zeroed, 1)
                norm_vector(nc, C, dve, ns)

                def layer_norm(n):
                    wait(dve, xT_psum, n)
                    normalized(nc, C, xn, n).then_inc(xn_ready, 1)

                def mix(n, par):
                    dve.wait_ge(xT_ready, n + 1)
                    wait(dve, mixed, 2 * n)
                    now, before = xT[par][:, :, 1:], xT[par][:, :, 0:P]
                    v.tensor_tensor(step_back[:], now, before, ALU.subtract).then_inc(back_ready, 1)
                    dve.wait_ge(back_ready, n + 1)
                    wait(dve, v_psum, n - 1)
                    for o, mu in ((xk, "mu_k"), (xr, "mu_r")):
                        v.scalar_tensor_tensor(out=o[par][:], in0=step_back[:], scalar=C.w(mu), in1=before,
                                               op0=ALU.mult, op1=ALU.add).then_inc(mixed, 1)

                def product(n, par):
                    dve.wait_ge(v_psum, n + 1)
                    dve.wait_ge(gates, n + 1)
                    wait(dve, finals, n - 1)
                    v.tensor_tensor(out[par][:], V[par][:, :].rearrange("p (b d) -> p b d", b=GB), gate[par][:], ALU.mult)\
                        .then_inc(products, 1)

                layer_norm(0)
                mix(0, 0)

                def group(n, par, first, last_group):
                    if not last_group:
                        layer_norm(n + 1)
                        mix(n + 1, 1 - par)
                    product(n, par)

                over_groups(dve, group)

            @block.gpsimd
            def _(pool):
                g = nc.gpsimd
                norm_pool(nc, C, pool, ns)

                def group(n, par, first, last_group):
                    pool.wait_ge(relus, n + 1)
                    wait(pool, v_psum, n)
                    g.tensor_tensor(kact[:], relu[:], relu[:], ALU.mult).then_inc(squares, 1)
                    if not first:
                        final(n - 1, 1 - par)

                def final(n, par):
                    pool.wait_ge(products, n + 1)
                    xg = C.x[:, batch(n, 0, GB), :]
                    g.tensor_tensor(xg, xg, out[par][:], ALU.add).then_inc(finals, 1)

                over_groups(pool, group)
                final(NG - 1, (NG - 1) % 2)

            @block.sync
            def _(sp):
                def group(n, par, first, last_group):
                    sp.wait_ge(finals, n + 1)
                    sp.dma_start(A["out"][:, batch(n, 0, GB), :], C.x[:, batch(n, 0, GB), :]).then_inc(stored, 16)

                over_groups(sp, group)
                sp.wait_ge(stored, 16 * NG)


def store(nc, C, A):
    with Phase(nc, "store") as ph:
        stored = ph.sem("stored")
        with nc.Block() as block:

            @block.sync
            def _(sp):
                sp.dma_start(A["out"], C.x[:]).then_inc(stored, 16)
                sp.wait_ge(stored, 16)


def diagonal(o):
    o = o.rearrange("k g (j c) -> k g j c", c=32)
    steps = [list(x) for x in o.ap]
    steps[2] = [steps[2][0] + DH, PART]
    steps[3] = [steps[3][0], DH]
    return bass.AP(tensor=o.tensor, offset=o.offset, ap=steps)


def program(nc, A, upto=99):
    with ExitStack() as stack:
        C = Chip()

        def sb(name, shape, dt=F32):
            return stack.enter_context(nc.sbuf_tensor(name, shape, dt))

        C.q_scratch = nc.dram_tensor("q_scratch", (2, P, GT), F16)
        C.k_scratch = nc.dram_tensor("k_scratch", (2, P, GK), F16)
        C.passed = stack.enter_context(nc.semaphore("passed"))
        C.bank = [stack.enter_context(nc.psum_tensor(f"bank{i}", [P, 512], F32)) for i in range(8)]
        C.x = sb("x_res", [P, NB, D])
        C.ctxT = sb("ctxT", [P, NB, TK])
        C.pack = sb("pack_sb", [P, PACK_COLS])
        C.rows = sb("rows_sb", [P, ROW_COLS])
        C.w = lambda name: C.pack[:, PACK[name][0]:PACK[name][0] + PACK[name][1]]
        C.row = lambda name: C.rows[:, ROWS[name][0]:ROWS[name][0] + ROWS[name][1]]
        C.stats = sb("stats", [P, NB, 6])
        C.norm_tmp = sb("norm_tmp", [P, 3, NB])
        C.rstd = sb("rstd", [P, NB])
        C.minus_half = sb("minus_half", [P, NB])
        C.shift = sb("shift", [P, NB])
        C.ident = sb("ident", [P, P])
        C.neg_ident = sb("neg_ident", [P, P], BF16)
        C.neg_big = sb("neg_big", [P, P], BF16)
        C.pos_big = sb("pos_big", [P, P], BF16)
        C.head_rows = sb("head_rows", [P, PART])
        C.head_cols = sb("head_cols", [P, PART, 32])
        C.mask2 = sb("mask2", [P, TK], BF16)
        C.mask2_less = sb("mask2_less", [P, TK], BF16)
        C.lowest2 = sb("lowest2", [P, 1], BF16)
        C.lens = sb("lens", [P, NB])
        C.key_row = sb("key_row", [P, TK])
        C.keep0 = sb("keep0", [P, NB])
        C.bias0 = sb("bias0", [P, NB])
        C.wquant = sb("wquant", [P, 9, P], BF16)
        C.wscale = sb("wscale_keep", [P, 9])
        C.down_scale = sb("down_scale", [P, D])
        C.route = sb("route", [P, LEAVES])
        C.leaf = sb("leaf", [P, 2, D])
        C.peak = sb("peak", [P, 4])
        C.scale = sb("act_scale", [P, 4])
        C.clip = sb("clip", [P, 2])
        with nc.sbuf_tensor("w1_sb", [P, E, FC, P], F32) as w1:
            C.w1 = w1
            setup(nc, C, A)
            if upto >= 1:
                attention(nc, C, 0, C.row("bf0"))
            if upto >= 2:
                experts(nc, C, A)
        if upto >= 3:
            attention(nc, C, 1, C.row("bv1"))
        if upto >= 4:
            quantized_gated(nc, C)
        if upto >= 5:
            attention(nc, C, 2, C.row("bo2"))
        if upto >= 6:
            tree(nc, C)
        if upto >= 7:
            attention(nc, C, 3, C.row("bp3"))
        if upto >= 8:
            channel_mix(nc, C, A)
            return
        store(nc, C, A)


OUT = ("out", (P, NB, D))


def layout(inputs):
    i = {k: np.asarray(v) for k, v in inputs.items()}
    perm = np.arange(D).reshape(PART, PART, DH).transpose(1, 0, 2).reshape(-1)
    col = lambda b: b.reshape(-1, 1)
    a = {}
    for l, (q, k, v) in enumerate((("L0_xattn_Wq", "L0_xattn_Wk", "L0_xattn_Wv"), ("L1_xattn_wq", "L1_xattn_wk", "L1_xattn_wv"),
                                   ("L2_xattn_wq", "L2_xattn_wk", "L2_xattn_wv"))):
        a[f"wq{l}"], a[f"wk{l}"], a[f"wv{l}"] = i[q][:, perm], i[k][:, perm], i[v]
        q, k, v = (n.replace("W", "b").replace("_w", "_b") for n in (q, k, v))
        a[f"bq{l}"], a[f"bk{l}"], a[f"bv{l}"] = col(i[q][perm]), col(i[k][perm]), col(i[v])
    a["wq3"], a["wk3"], a["wv3"] = i["L3_xattn_w_attn"][:, perm], i["L3_xattn_w_vis"][:, perm], i["L3_xattn_w_vis"]
    a["bq3"], a["bk3"], a["bv3"] = (col(i["L3_xattn_b_attn"][perm]), col(i["L3_xattn_b_vis"][perm]), col(i["L3_xattn_b_vis"]))
    a["wo0"], a["wo2"], a["wo3"] = i["L0_xattn_Wf"], i["L2_xattn_wo"], i["L3_xattn_w_proj"]
    a["choice"] = i["L0_ffn_choice"].T

    def rows_in_chunks(w):
        w = np.concatenate([w, np.zeros((3 * P - I1, D), w.dtype)])
        return w.reshape(3, P, D).transpose(1, 0, 2).reshape(P, 3 * D)

    a["gate"], a["up"] = rows_in_chunks(i["L1_ffn_w_gate"]), rows_in_chunks(i["L1_ffn_w_up"])
    a["down"] = np.concatenate([i["L1_ffn_w_down"], np.zeros((D, 3 * P - I1), np.float32)], axis=1)
    a["tree_q"] = i["L2_ffn_Wq"]
    a["routers"] = np.concatenate([i["L2_ffn_routers"], np.zeros((1, D), np.float32)]).T
    a["leaves"], a["tree_out"] = i["L2_ffn_leaf_values"].T, i["L2_ffn_Wout_w"].T
    a["mix_r"], a["mix_k"], a["mix_v"] = i["L3_ffn_W_r"].T, i["L3_ffn_W_k"].T, i["L3_ffn_W_v"].T
    a["mu_r"], a["mu_k"] = col(i["L3_ffn_mu_r"]), col(i["L3_ffn_mu_k"])
    rows = {"bf0": i["L0_xattn_bf"], "bv1": i["L1_xattn_bv"], "bo2": i["L2_xattn_bo"], "bp3": i["L3_xattn_b_proj"],
            "tree_b": i["L2_ffn_Wout_b"], "clip_x": i["L1_ffn_clip_x"], "clip_down": i["L1_ffn_clip_down"]}
    return {
        "x": i["x"].transpose(1, 0, 2),
        "ctx": i["ctx_1024"].transpose(2, 0, 1),
        "pack": np.concatenate([a[n] for n in PACK], axis=1),
        "rows": np.concatenate([rows[n] for n in ROWS]).reshape(1, ROW_COLS),
        "lens": i["_lenS2"].reshape(1, NB),
        "mask": i["mask_1x1xSxS2_fk1"].reshape(P, TK),
        "w1": i["L0_ffn_W1"].reshape(E, D, FC, P).transpose(1, 0, 2, 3),
        "w2": i["L0_ffn_W2"].reshape(E, FC, P, D).transpose(2, 0, 1, 3),
    }


def kernel(**inputs):
    import concourse.bacc as bacc
    from concourse.bass_utils import run_bass_kernel_spmd

    nc = bacc.Bacc("TRN2", target_bir_lowering=False, num_devices=1)
    arrays = {f"in_{n}": np.ascontiguousarray(a) for n, a in layout(inputs).items()}
    A = {n[3:]: nc.dram_tensor(n, a.shape, mybir.dt.from_np(a.dtype), kind="ExternalInput").ap() for n, a in arrays.items()}
    A["out"] = nc.dram_tensor(OUT[0], OUT[1], F32, kind="ExternalOutput").ap()
    program(nc, A)
    r = run_bass_kernel_spmd(nc, [arrays], core_ids=[0])
    return np.ascontiguousarray(r.results[0][OUT[0]].transpose(1, 0, 2))
```

```python
from contextlib import ExitStack

import numpy as np
import concourse.bass as bass
from concourse import mybir

F32 = mybir.dt.float32
F16 = mybir.dt.float16
BF16 = mybir.dt.bfloat16
I32 = mybir.dt.int32
U16 = mybir.dt.uint16
ALU = mybir.AluOpType
ACT = mybir.ActivationFunctionType
AX = mybir.AxisListType

P = 128
NB = 64
TK = 120
D = 128
HEADS = 16
DH = D // HEADS
PART = 4
GB = 4
NG = NB // GB
SLOTS = GB * PART
GT = GB * P
GK = GB * TK
E = 8
FC = 4
I1 = 352
IC = [(0, 128), (128, 128), (256, 96)]
LEAVES = 256
LIFT = 32.0
X_LIFT = 1024.0
H_LIFT = 64.0
W_LIFT = 1024.0
BIG = 998244352.0
MAGIC = 12582912.0
EPS = 1e-5
QMAX = 127.0

PACK = {}
PACK_COLS = 0
for _name, _n in ([(f"w{k}{l}", D) for l in range(4) for k in "qkv"] + [(f"wo{l}", D) for l in (0, 2, 3)]
                  + [(f"b{k}{l}", 1) for l in range(4) for k in "qkv"]
                  + [("choice", E), ("gate", 3 * D), ("up", 3 * D), ("down", 3 * P), ("tree_q", D),
                     ("routers", LEAVES), ("leaves", LEAVES), ("tree_out", D), ("mix_r", D), ("mix_k", D),
                     ("mix_v", D), ("mu_r", 1), ("mu_k", 1)]):
    PACK[_name] = (PACK_COLS, _n)
    PACK_COLS += _n
ROWS = {"bf0": (0, D), "bv1": (D, D), "bo2": (2 * D, D), "bp3": (3 * D, D), "tree_b": (4 * D, D),
        "clip_x": (5 * D, 1), "clip_down": (5 * D + 1, 1)}
ROW_COLS = 5 * D + 2


def wait(eng, sem, value):
    if isinstance(value, int) and value <= 0:
        return
    eng.wait_ge(sem, value)


def apart(eng, C):
    eng.sem_inc(C.passed, 1)


def over_groups(eng, body):
    body(0, 0, True, False)
    body(1, 1, False, False)
    with eng.Fori(0, (NG - 4) // 2) as i:
        body(i * 2 + 2, 0, False, False)
        body(i * 2 + 3, 1, False, False)
    body(NG - 2, (NG - 2) % 2, False, False)
    body(NG - 1, (NG - 1) % 2, False, True)


class Chip:
    pass


class Phase:

    def __init__(self, nc, name):
        self.nc, self.name, self.stack, self.sems = nc, name, ExitStack(), []

    def __enter__(self):
        self.stack.__enter__()
        return self

    def __exit__(self, *a):
        self.nc.clear_and_free_semaphores(self.sems)
        self.nc.all_engine_barrier()
        return self.stack.__exit__(*a)

    def sb(self, name, shape, dt=F32):
        return self.stack.enter_context(self.nc.sbuf_tensor(f"{self.name}_{name}", shape, dt))

    def sem(self, name):
        self.sems.append(self.nc.alloc_semaphore(f"{self.name}_{name}"))
        return self.sems[-1]


class Chain:

    def __init__(self, eng, sem):
        self.eng, self.sem, self.n = eng, sem, 0

    def __call__(self, ins):
        self.n += 1
        ins.then_inc(self.sem, 1)
        self.eng.wait_ge(self.sem, self.n)


def batch(t, b, n=1):
    return bass.ds(t * GB + b, n)



NORM_STEPS = 11


def norm_vector(nc, C, dve, ph):
    ch = Chain(dve, ph["norm_step"])
    st = C.stats
    t = C.norm_tmp
    ch(nc.vector.tensor_tensor(t[:, 0], st[:, :, 1], st[:, :, 4], ALU.add))
    ch(nc.vector.tensor_tensor(t[:, 1], st[:, :, 1], st[:, :, 4], ALU.subtract))
    ch(nc.vector.tensor_tensor(t[:, 2], st[:, :, 2], st[:, :, 5], ALU.add))
    ch(nc.vector.tensor_tensor(t[:, 1], t[:, 1], t[:, 1], ALU.mult))
    ch(nc.vector.scalar_tensor_tensor(out=t[:, 2], in0=t[:, 1], scalar=D / 4.0, in1=t[:, 2], op0=ALU.mult, op1=ALU.add))
    nc.vector.tensor_scalar(t[:, 1], t[:, 2], 1.0 / D, EPS, ALU.mult, ALU.add).then_inc(ph["var_ready"], 1)
    dve.wait_ge(ph["root_ready"], 1)
    ch(nc.vector.reciprocal(C.rstd[:], t[:, 2]))
    ch(nc.vector.tensor_tensor(t[:, 2], t[:, 1], C.rstd[:], ALU.mult))
    ch(nc.vector.tensor_tensor(t[:, 2], t[:, 2], C.rstd[:], ALU.mult))
    ch(nc.vector.tensor_scalar(t[:, 2], t[:, 2], -0.5, 1.5, ALU.mult, ALU.add))
    ch(nc.vector.tensor_tensor(C.rstd[:], C.rstd[:], t[:, 2], ALU.mult))
    ch(nc.vector.scalar_tensor_tensor(out=C.shift[:], in0=t[:, 0], scalar=-0.5, in1=C.rstd[:], op0=ALU.mult, op1=ALU.mult))


def norm_root(nc, C, act, ph):
    act.wait_ge(ph["var_ready"], 1)
    nc.scalar.activation(C.norm_tmp[:, 2], C.norm_tmp[:, 1], ACT.Sqrt).then_inc(ph["root_ready"], 1)


def norm_sems(ph):
    return {n: ph.sem(n) for n in ("norm_step", "var_ready", "root_ready")}


def normalized(nc, C, out, n):
    for b in range(GB):
        last = nc.vector.tensor_scalar(out[:, b:b + 1, :], C.x[:, batch(n, b), :], C.rstd[:, batch(n, b)],
                                       C.shift[:, batch(n, b)], ALU.mult, ALU.add)
    return last



def setup(nc, C, A):
    with Phase(nc, "setup") as ph:
        pack_in, rows_in, len_in, mask_in = (ph.sem(n) for n in ("pack_in", "rows_in", "len_in", "mask_in"))
        nx = 4
        x_in = [ph.sem(f"x{k}_in") for k in range(nx)]
        pool_step, dve_step, made, folded_ready, psum_ready, psum_read, quantized = (
            ph.sem(n) for n in ("pool_step", "dve_step", "made", "folded_ready", "psum_ready", "psum_read", "quantized"))
        lens_i = ph.sb("lens_i", [P, NB], I32)
        lens = ph.sb("lens", [P, NB])
        len0 = ph.sb("len0", [P, NB])
        key_col = ph.sb("key_col", [P, 1])
        mask_f = ph.sb("mask_f", [P, TK])
        lowest = ph.sb("lowest", [P, 1])
        ones = ph.sb("ones", [P, P])
        wabs = ph.sb("wabs", [P, 9])
        wscale = ph.sb("wscale", [P, 9])
        winv = ph.sb("winv", [P, 9])
        wint = ph.sb("wint", [P, 9, D])
        diag = ph.sb("diag", [P, P])
        with nc.Block() as block:

            @block.sync
            def _(sp):
                sp.dma_start(C.rows[:], A["rows"].to_broadcast([P, ROW_COLS])).then_inc(rows_in, 16)
                sp.dma_start(lens_i[:], A["lens"].to_broadcast([P, NB])).then_inc(len_in, 16)
                sp.dma_start(mask_f[:], A["mask"]).then_inc(mask_in, 16)
                for k in range(nx):
                    s = slice(k * NB // nx, (k + 1) * NB // nx)
                    sp.dma_start(C.x[:, s, :], A["x"][:, s, :]).then_inc(x_in[k], 16)
                sp.dma_start(C.pack[:], A["pack"]).then_inc(pack_in, 16)
                for k in range(2):
                    s = slice(k * NB // 2, (k + 1) * NB // 2)
                    sp.dma_start(C.ctxT[:, s, :], A["ctx"][:, s, :]).then_inc(C.ctx_in, 16)
                sp.dma_start(C.w1[:], A["w1"]).then_inc(C.w1_in, 16)

            @block.gpsimd
            def _(pool):
                ch = Chain(pool, pool_step)

                def keep_where(t, value, pattern, base, cm, op):
                    ch(nc.gpsimd.affine_select(out=t, in_=t, compare_op=op, fill=value, base=base,
                                               pattern=pattern, channel_multiplier=cm))
                for t, v in ((C.ident, 1.0), (C.neg_ident, -1.0), (C.neg_big, -BIG * LIFT * LIFT), (C.pos_big, BIG * LIFT * LIFT)):
                    ch(nc.gpsimd.memset(t[:], v))
                    keep_where(t[:], 0.0, [[-1, P]], 0, 1, ALU.is_equal)
                ch(nc.gpsimd.memset(C.head_rows[:], 1.0))
                for p in range(PART):
                    t = C.head_rows[32 * p:32 * p + 32, :]
                    keep_where(t, 0.0, [[-DH, PART]], 0, 1, ALU.is_ge)
                    keep_where(t, 0.0, [[DH, PART]], DH - 1, -1, ALU.is_ge)
                ch(nc.gpsimd.memset(C.head_cols[:], 1.0))
                keep_where(C.head_cols[:], 0.0, [[-DH, PART], [1, 32]], 0, 0, ALU.is_ge)
                keep_where(C.head_cols[:], 0.0, [[DH, PART], [-1, 32]], DH - 1, 0, ALU.is_ge)
                ch(nc.gpsimd.memset(ones[:], 1.0))
                ch(nc.gpsimd.iota(C.key_row[:], pattern=[[1, TK]], base=0, channel_multiplier=0,
                                  allow_small_or_imprecise_dtypes=True))
                ch(nc.gpsimd.iota(key_col[:], pattern=[[0, 1]], base=0, channel_multiplier=1,
                                  allow_small_or_imprecise_dtypes=True))
                pool.sem_inc(made, 1)

            @block.vector
            def _(dve):
                ch = Chain(dve, dve_step)
                v = nc.vector
                for b in range(NB):
                    if b % (NB // nx) == 0:
                        dve.wait_ge(x_in[b // (NB // nx)], 16)
                    last = v.bn_stats(C.stats[:, b, :], C.x[:, b, :])
                ch(last)
                dve.wait_ge(len_in, 16)
                dve.wait_ge(made, 1)
                ch(v.tensor_copy(lens[:], lens_i[:]))
                ch(v.tensor_scalar(len0[:], lens[:], 0.0, None, ALU.is_gt))
                ch(v.tensor_scalar(C.keep0[:], len0[:], LIFT ** -2, None, ALU.mult))
                ch(v.tensor_scalar(C.bias0[:], lens[:], key_col[:], -1e30, ALU.is_le, ALU.mult))
                ch(v.tensor_tensor(C.bias0[:], C.bias0[:], len0[:], ALU.mult))
                ch(v.tensor_scalar(len0[:], len0[:], -float(TK), float(TK), ALU.mult, ALU.add))
                ch(v.tensor_tensor(C.lens[:], lens[:], len0[:], ALU.max))
                dve.wait_ge(mask_in, 16)
                ch(v.tensor_reduce(lowest[:], mask_f[:], AX.X, ALU.min))
                ch(v.tensor_copy(C.lowest2[:], lowest[:]))
                ch(v.tensor_copy(C.mask2[:], mask_f[:]))
                ch(v.tensor_scalar(C.mask2_less[:], mask_f[:], lowest[:], None, ALU.subtract))
                dve.wait_ge(pack_in, 16)
                for l in range(4):
                    for w in (C.w(f"wq{l}"), C.w(f"bq{l}")):
                        ch(v.tensor_scalar(w, w, LIFT * float(DH) ** -0.5, None, ALU.mult))
                    ch(v.tensor_scalar(C.w(f"bk{l}"), C.w(f"bk{l}"), LIFT, None, ALU.mult))
                for k, name in enumerate(("gate", "up", "down")):
                    m = C.w(name).rearrange("p (c d) -> p c d", c=3)
                    if name == "down":
                        ch(v.tensor_reduce(wabs[:, 6:7], C.w(name)[:, 0:I1], AX.X, ALU.max, apply_absolute_value=True))
                        for c in (7, 8):
                            ch(v.tensor_copy(wabs[:, c:c + 1], wabs[:, 6:7]))
                    else:
                        ch(v.tensor_reduce(wabs[:, 3 * k:3 * k + 3], m, AX.X, ALU.max, apply_absolute_value=True))
                ch(v.tensor_scalar(wscale[:], wabs[:], 1.0 / QMAX, None, ALU.mult))
                ch(v.tensor_copy(C.wscale[:], wscale[:]))
                ch(v.tensor_scalar(wscale[:], wscale[:], 1e-30, None, ALU.max))
                ch(v.reciprocal(winv[:], wscale[:]))
                for k, name in enumerate(("gate", "up", "down")):
                    m = C.w(name).rearrange("p (c d) -> p c d", c=3)
                    for c in range(3):
                        q = wint[:, 3 * k + c, :]
                        ch(v.tensor_scalar(q, m[:, c, :], winv[:, 3 * k + c:3 * k + c + 1], MAGIC, ALU.mult, ALU.add))
                        ch(v.tensor_scalar(q, q, MAGIC, -QMAX - 1.0, ALU.subtract, ALU.max))
                        ch(v.tensor_scalar(q, q, QMAX, None, ALU.min))
                ch(v.tensor_scalar(diag[:], C.ident[:], C.wscale[:, 6:7], None, ALU.mult))
                dve.sem_inc(quantized, 1)
                dve.wait_ge(rows_in, 16)
                for k, name in enumerate(("bf0", "bo2", "bp3")):
                    dve.wait_ge(folded_ready, k + 1)
                    r = C.row(name)
                    ch(v.tensor_tensor(r, C.bank[k][:, 0:D], r, ALU.add))

            @block.tensor
            def _(pe):
                t = nc.tensor
                pe.wait_ge(made, 1)
                pe.wait_ge(pack_in, 16)
                for k, l in enumerate((0, 2, 3)):
                    t.matmul(C.bank[k][:, 0:D], C.w(f"bv{l}").to_broadcast([P, P]), C.w(f"wo{l}"),
                             start=True, stop=True).then_inc(folded_ready, 1)
                t.matmul(C.bank[3][:, 0:LEAVES], C.w("tree_q"), C.w("routers"), start=True, stop=True).then_inc(psum_ready, 1)
                for c in range(2):
                    o = PACK["leaves"][0] + P * c
                    t.matmul(C.bank[4 + c][:, 0:D], C.pack[:, o:o + P], C.w("tree_out"),
                             start=True, stop=True).then_inc(psum_ready, 1)
                pe.wait_ge(quantized, 1)
                for k in range(9):
                    if k >= 2:
                        pe.wait_ge(psum_read, 3 + k - 1)
                    t.transpose(C.bank[6 + k % 2][:, 0:P], wint[:, k, :], C.ident[:]).then_inc(psum_ready, 1)
                pe.wait_ge(psum_read, 3 + 8)
                t.matmul(C.bank[7][:, 128:256], ones[:], diag[:], start=True, stop=True).then_inc(psum_ready, 1)

            @block.scalar
            def _(act):
                a = nc.scalar
                act.wait_ge(psum_ready, 1)
                a.activation(C.route[:], C.bank[3][:, 0:LEAVES], ACT.Copy).then_inc(psum_read, 1)
                for c in range(2):
                    act.wait_ge(psum_ready, 2 + c)
                    a.activation(C.leaf[:, c, :], C.bank[4 + c][:, 0:D], ACT.Copy).then_inc(psum_read, 1)
                for k in range(9):
                    act.wait_ge(psum_ready, 4 + k)
                    a.activation(C.wquant[:, k, :], C.bank[6 + k % 2][:, 0:P], ACT.Copy).then_inc(psum_read, 1)
                act.wait_ge(psum_ready, 13)
                a.activation(C.down_scale[:], C.bank[7][:, 128:256], ACT.Copy).then_inc(psum_read, 1)
                act.wait_ge(psum_read, 13)



def attention(nc, C, l, bias_row):
    masked = {0: "lengths", 2: "mask"}.get(l)
    with Phase(nc, f"att{l}") as ph:
        xn = ph.sb("xn", [P, GB, D])
        xnT = ph.sb("xnT", [P, GT])
        q_full = ph.sb("q_full", [P, GT])
        k_full = ph.sb("k_full", [P, GK])
        q_part = ph.sb("q_part", [P, 2, GT], F16)
        k_part = ph.sb("k_part", [P, 2, GK], F16)
        q_stack = ph.sb("q_stack", [P, PART, GT], F16)
        q_block = [ph.sb(f"q_block{i}", [P, PART, PART, GT], F16) for i in range(2)]
        k_stack = [ph.sb(f"k_stack{i}", [P, PART, GK], F16) for i in range(2)]
        ctx = ph.sb("ctx", [P, GK])
        v_pad = [ph.sb(f"v_pad{i}", [P, GB, PART, PART, 32]) for i in range(2)]
        probs = [ph.sb(f"probs{i}", [P, PART, P]) for i in range(4)]
        top = ph.sb("top", [P, SLOTS, PART], BF16)
        inv_sum = ph.sb("inv_sum", [P, P])
        heads_out = [ph.sb(f"heads_out{i}", [P, P]) for i in range(2)]
        x_bias = [ph.sb(f"x_bias{i}", [P, GB, D]) for i in range(2)]
        S = C.bank[0:2]
        ST = C.bank[2:4]
        SUMS, OUT, PREP = C.bank[4:6], C.bank[6], C.bank[7]
        if masked == "lengths":
            mask0 = ph.sb("mask0", [P, GB, TK], U16)
            key0 = ph.sb("key0", [P, GB])
        ns = norm_sems(ph)
        (xn_ready, xnT_psum, xnT_ready, q_psum, q_read, k_psum, k_read, v_psum, v_read, q_split, k_split, q_stacked,
         k_stacked, q_blocked, ctx_ready, scores, maxed, shifted, exps, weighed, inv_ready, normed, out_psum, added,
         xb_ready, padded, mask_ready, k_masked, k_hi, q_spilled, k_spilled) = (ph.sem(n) for n in (
             "xn_ready", "xnT_psum", "xnT_ready", "q_psum", "q_read", "k_psum", "k_read", "v_psum", "v_read", "q_split",
             "k_split", "q_stacked", "k_stacked", "q_blocked", "ctx_ready", "scores", "maxed", "shifted", "exps",
             "weighed", "inv_ready", "normed", "out_psum", "added", "xb_ready", "padded", "mask_ready", "k_masked", "k_hi",
             "q_spilled", "k_spilled"))
        wk = C.w(f"wk{l}")
        NQ = PART * 16

        with nc.Block() as block:

            @block.tensor
            def _(pe):
                t = nc.tensor

                def form_scores(n, s, par):
                    b, j = s // PART, s % PART
                    wait(pe, maxed, 16 * n + s - 1)
                    if s == 0:
                        pe.wait_ge(q_blocked, PART * (n + 1))
                        pe.wait_ge(k_stacked, NQ * (n + 1))
                    o = S[s % 2][:, 0:GK].rearrange("p (g k) -> p g k", g=PART)
                    if masked == "mask":
                        t.matmul(o, C.neg_big[:], C.mask2_less[:].unsqueeze(1).to_broadcast([P, PART, TK]),
                                 start=True, stop=False)
                    for g in range(PART):
                        last = t.matmul(o[:, g, :], q_block[par][:, j, g, b * P:(b + 1) * P],
                                        k_stack[par][:, j, b * TK:(b + 1) * TK],
                                        start=masked != "mask", stop=masked != "mask" or g == PART - 1)
                    last.then_inc(scores, 1)

                def form_shifted(n, s, par):
                    b, j = s // PART, s % PART
                    wait(pe, exps, 16 * n + s - 1)
                    o = ST[s % 2][0:TK, :].rearrange("k (g q) -> k g q", g=PART)
                    t.matmul(o, k_stack[par][:, j, b * TK:(b + 1) * TK], q_block[par][:, j, :, b * P:(b + 1) * P],
                             start=True, stop=False)
                    if masked == "mask":
                        t.matmul(o, C.mask2[:], C.neg_big[:].unsqueeze(1).to_broadcast([P, PART, P]), start=False, stop=False)
                        t.matmul(o, C.lowest2[:].to_broadcast([P, TK]), C.pos_big[:].unsqueeze(1).to_broadcast([P, PART, P]),
                                 start=False, stop=False)
                    wait(pe, maxed, 16 * n + s + 1)
                    for g in range(PART):
                        last = t.matmul(o[:, g, :], top[:, s, g:g + 1].to_broadcast([P, TK]), C.neg_ident[:],
                                        start=False, stop=g == PART - 1)
                    last.then_inc(shifted, 1)

                def weigh(n, s, par):
                    b, j = s // PART, s % PART
                    pe.wait_ge(exps, 16 * n + s + 1)
                    if j == 0:
                        wait(pe, normed, 4 * n + b - 1)
                        if b == 0:
                            pe.wait_ge(v_read, n + 1)
                    p, o = probs[s % 4], SUMS[b % 2]
                    for g in range(PART):
                        t.matmul(o[32 * g:32 * g + 32, 0:P], v_pad[par][0:TK, b, g, j, :], p[0:TK, g, :],
                                 start=j == 0, stop=False)
                    for g in range(PART):
                        last = t.matmul(o[32 * g:32 * g + 32, P:2 * P], C.head_cols[0:TK, j, :], p[0:TK, g, :],
                                        start=False, stop=j == PART - 1)
                    last.then_inc(weighed, 1)

                def project_out(n, b):
                    pe.wait_ge(normed, 4 * n + b + 1)
                    wait(pe, added, 4 * n + b)
                    if l == 1:
                        t.transpose(OUT[:, 0:D], heads_out[b % 2][:], C.ident[:]).then_inc(out_psum, 1)
                    else:
                        t.matmul(OUT[:, 0:D], heads_out[b % 2][:], C.w(f"wo{l}"), start=True, stop=True).then_inc(out_psum, 1)

                def prepare(n, step):
                    if step == 0:
                        pe.wait_ge(xn_ready, 2 * n + 2)
                        wait(pe, v_read, n)
                        for b in range(GB):
                            last = t.transpose(PREP[:, b * P:(b + 1) * P], xn[:, b, :], C.ident[:])
                        last.then_inc(xnT_psum, 1)
                    if step == 1:
                        pe.wait_ge(xnT_ready, n + 1)
                        t.matmul(PREP[:, :], C.w(f"wq{l}"), xnT[:], start=True, stop=True).then_inc(q_psum, 1)
                    if step == 2:
                        pe.wait_ge(q_read, n + 1)
                        pe.wait_ge(ctx_ready, n + 1)
                        t.matmul(PREP[:, 0:GK], wk, ctx[:], start=True, stop=True).then_inc(k_psum, 1)
                    if step == 3:
                        pe.wait_ge(k_read, n + 1)
                        for b in range(GB):
                            last = t.matmul(PREP[0:TK, b * D:(b + 1) * D], ctx[:, b * TK:(b + 1) * TK], C.w(f"wv{l}"),
                                            start=True, stop=True)
                        last.then_inc(v_psum, 1)

                for step in range(4):
                    prepare(0, step)
                for s in range(2):
                    form_scores(0, s, 0)

                def group(n, par, first, last_group):
                    for s in range(SLOTS):
                        form_shifted(n, s, par)
                        if s + 2 < SLOTS:
                            form_scores(n, s + 2, par)
                        elif not last_group:
                            form_scores(n + 1, s + 2 - SLOTS, 1 - par)
                        if s > 0:
                            weigh(n, s - 1, par)
                        elif not first:
                            weigh(n - 1, SLOTS - 1, 1 - par)
                        if s % PART == 2 and not (first and s == 2):
                            if s == 2:
                                project_out(n - 1, GB - 1)
                            else:
                                project_out(n, s // PART - 1)
                        if s % 2 == 0 and s <= 6 and not last_group:
                            prepare(n + 1, s // 2)

                over_groups(pe, group)
                weigh(NG - 1, SLOTS - 1, (NG - 1) % 2)
                project_out(NG - 1, GB - 1)

            @block.scalar
            def _(act):
                a = nc.scalar

                def read_prepared(n, step, par):
                    if step == 0:
                        act.wait_ge(xnT_psum, n + 1)
                        wait(act, q_psum, n)
                        a.activation(xnT[:], PREP[:, :], ACT.Copy).then_inc(xnT_ready, 1)
                    if step == 1:
                        act.wait_ge(q_psum, n + 1)
                        wait(act, q_split, n)
                        wait(act, q_spilled, 16 * n)
                        a.activation(q_full[:], PREP[:, :], ACT.Identity, bias=C.w(f"bq{l}"))
                        a.activation(q_part[:, 0, :], PREP[:, :], ACT.Identity, bias=C.w(f"bq{l}")).then_inc(q_read, 1)
                    if step == 2:
                        act.wait_ge(k_psum, n + 1)
                        wait(act, k_split, n)
                        wait(act, k_spilled, 16 * n)
                        last = a.activation(k_full[:], PREP[:, 0:GK], ACT.Identity, bias=C.w(f"bk{l}"), scale=LIFT)
                        if masked == "lengths":
                            last = a.activation(key0[:], PREP[:, 0:GK].rearrange("p (b k) -> p b k", b=GB)[:, :, 0], ACT.Identity,
                                                bias=C.w(f"bk{l}"), scale=LIFT)
                        else:
                            last = a.activation(k_part[:, 0, :], PREP[:, 0:GK], ACT.Identity, bias=C.w(f"bk{l}"), scale=LIFT)
                        last.then_inc(k_read, 1)
                    if step == 3:
                        act.wait_ge(v_psum, n + 1)
                        wait(act, weighed, 16 * (n - 1))
                        if isinstance(n, int) and n < 2:
                            act.wait_ge(padded, 2)
                        for b in range(GB):
                            o = v_pad[par][0:TK, b, :, :, :].rearrange("k g j c -> k g (j c)")
                            o = diagonal(o)
                            last = a.activation(o, PREP[0:TK, b * D:(b + 1) * D].rearrange("k (g j d) -> k g j d", g=PART, j=PART),
                                                ACT.Copy)
                        last.then_inc(v_read, 1)

                def exponential(n, s):
                    act.wait_ge(shifted, 16 * n + s + 1)
                    wait(act, weighed, 16 * n + s - 3)
                    o, i = probs[s % 4][0:TK, :, :], ST[s % 2][0:TK, :].rearrange("k (g q) -> k g q", g=PART)
                    if masked == "lengths":
                        b = s // PART
                        apart(act, C)
                        last = a.activation(o, i, ACT.Exp, bias=C.bias0[0:TK, batch(n, b)], scale=C.keep0[0:TK, batch(n, b)])
                    else:
                        last = a.activation(o, i, ACT.Exp, scale=LIFT ** -2)
                    last.then_inc(exps, 1)

                norm_root(nc, C, act, ns)

                def high_keys(n):
                    act.wait_ge(k_masked, n + 1)
                    a.activation(k_part[:, 0, :], k_full[:], ACT.Copy).then_inc(k_hi, 1)

                for step in range(4):
                    read_prepared(0, step, 0)
                    if step == 2 and masked == "lengths":
                        high_keys(0)

                def group(n, par, first, last_group):
                    for s in range(SLOTS):
                        exponential(n, s)
                        if s % 2 == 0 and s <= 6 and not last_group:
                            read_prepared(n + 1, s // 2, 1 - par)
                        if s == 5 and masked == "lengths" and not last_group:
                            high_keys(n + 1)

                over_groups(act, group)

            @block.vector
            def _(dve):
                v = nc.vector
                norm_vector(nc, C, dve, ns)

                def maximum(n, s):
                    dve.wait_ge(scores, 16 * n + s + 1)
                    wait(dve, shifted, 16 * n + s - 15)
                    v.tensor_reduce(top[:, s, :], S[s % 2][:, 0:GK].rearrange("p (g k) -> p g k", g=PART), AX.X, ALU.max)\
                        .then_inc(maxed, 1)

                def normalize(n, b):
                    dve.wait_ge(weighed, 16 * n + 4 * (b + 1))
                    v.reciprocal(inv_sum[:], SUMS[b % 2][:, P:2 * P]).then_inc(inv_ready, 1)
                    dve.wait_ge(inv_ready, 4 * n + b + 1)
                    wait(dve, out_psum, 4 * n + b - 1)
                    v.tensor_tensor(heads_out[b % 2][:], SUMS[b % 2][:, 0:P], inv_sum[:], ALU.mult).then_inc(normed, 1)

                def add(n, b, par):
                    if b == 0:
                        dve.wait_ge(xb_ready, n + 1)
                    dve.wait_ge(out_psum, 4 * n + b + 1)
                    v.tensor_tensor(C.x[:, batch(n, b), :], OUT[:, 0:D].unsqueeze(1), x_bias[par][:, b:b + 1, :], ALU.add)\
                        .then_inc(added, 1)

                def statistics(n, b):
                    dve.wait_ge(added, 4 * n + b + 1)
                    return v.bn_stats(C.stats[:, batch(n, b), :], C.x[:, batch(n, b), :])

                def layer_norm(n, half):
                    if half == 0:
                        wait(dve, xnT_psum, n)
                    for b in (2 * half, 2 * half + 1):
                        last = v.tensor_scalar(xn[:, b:b + 1, :], C.x[:, batch(n, b), :], C.rstd[:, batch(n, b)],
                                               C.shift[:, batch(n, b)], ALU.mult, ALU.add)
                    last.then_inc(xn_ready, 1)

                def block_out(n, g, par):
                    if g == 0:
                        dve.wait_ge(q_stacked, NQ * (n + 1))
                        wait(dve, shifted, 16 * (n - 1))
                    v.tensor_scalar(q_block[par][:, :, g, :], q_stack[:], C.head_rows[:, g:g + 1], None, ALU.mult)\
                        .then_inc(q_blocked, 1)

                def key_masks(n):
                    wait(dve, k_masked, n)
                    apart(dve, C)
                    for b in range(GB):
                        last = v.tensor_scalar(mask0[:, b, :], C.key_row[:], C.lens[:, batch(n, b)], None, ALU.is_ge)
                    last.then_inc(mask_ready, 1)

                def replace_keys(n):
                    dve.wait_ge(k_read, n + 1)
                    dve.wait_ge(mask_ready, n + 1)
                    apart(dve, C)
                    v.copy_predicated(k_full[:].rearrange("p (b k) -> p b k", b=GB), mask0[:],
                                      key0[:].unsqueeze(2).to_broadcast([P, GB, TK])).then_inc(k_masked, 1)

                for half in range(2):
                    layer_norm(0, half)
                if masked == "lengths":
                    key_masks(0)
                for half in range(2):
                    layer_norm(1, half)
                if masked == "lengths":
                    replace_keys(0)
                for g in range(PART):
                    block_out(0, g, 0)
                for s in range(2):
                    maximum(0, s)

                def group(n, par, first, last_group):
                    for s in range(SLOTS):
                        if s == 2 and masked == "lengths" and not last_group:
                            key_masks(n + 1)
                        if s + 2 < SLOTS:
                            maximum(n, s + 2)
                        elif not last_group:
                            maximum(n + 1, s + 2 - SLOTS)
                        b = s // PART - 1
                        if 9 <= s <= 11 and not last_group:
                            block_out(n + 1, s - 9, 1 - par)
                        if s % PART == 0 and not (first and b < 0):
                            normalize(*((n - 1, GB - 1) if b < 0 else (n, b)))
                        if s == 4 and masked == "lengths" and not last_group:
                            replace_keys(n + 1)
                        if s % PART == 3 and not (first and b < 0):
                            add(*((n - 1, GB - 1, 1 - par) if b < 0 else (n, b, par)))
                            statistics(*((n - 1, GB - 1) if b < 0 else (n, b)))
                        if s in (5, 6) and not (isinstance(n, int) and n + 2 >= NG):
                            layer_norm(n + 2, s - 5)

                over_groups(dve, group)
                normalize(NG - 1, GB - 1)
                add(NG - 1, GB - 1, (NG - 1) % 2)
                statistics(NG - 1, GB - 1)

            @block.gpsimd
            def _(pool):
                g = nc.gpsimd
                for i in range(2):
                    g.memset(v_pad[i][:], 0.0).then_inc(padded, 1)

                def split(n, full, part, ready, done):
                    pool.wait_ge(ready, n + 1)
                    apart(pool, C)
                    g.tensor_tensor(part[:, 1, :], full[:], part[:, 0, :], ALU.subtract).then_inc(done, 1)

                pool.wait_ge(C.ctx_in, 32)

                def group(n, par, first, last_group):
                    wait(pool, v_psum, n)
                    apart(pool, C)
                    g.tensor_copy(ctx[:].rearrange("p (b k) -> p b k", b=GB), C.ctxT[:, batch(n, 0, GB), :]).then_inc(ctx_ready, 1)
                    split(n, q_full, q_part, q_read, q_split)
                    split(n, k_full, k_part, k_hi if masked == "lengths" else k_read, k_split)
                    wait(pool, added, 4 * (n - 1))
                    g.tensor_tensor(x_bias[par][:], C.x[:, batch(n, 0, GB), :],
                                    bias_row.unsqueeze(1).to_broadcast([P, GB, D]), ALU.add).then_inc(xb_ready, 1)
                    if not first:
                        pool.wait_ge(q_stacked, NQ * (n + 1))
                        wait(pool, shifted, 16 * (n - 1))
                        apart(pool, C)
                        g.tensor_scalar(q_block[par][:, :, PART - 1, :], q_stack[:], C.head_rows[:, PART - 1:PART], None, ALU.mult)\
                            .then_inc(q_blocked, 1)

                over_groups(pool, group)

            @block.sync
            def _(sp):
                def restack(n, part, split_done, scratch, spilled, stack, stacked, halves, free):
                    sp.wait_ge(split_done, n + 1)
                    apart(sp, C)
                    sp.dma_start(scratch[:, :, :].rearrange("h f t -> f h t"), part[:]).then_inc(spilled, 16)
                    sp.wait_ge(spilled, 16 * (n + 1))
                    apart(sp, C)
                    wait(sp, *free)
                    apart(sp, C)
                    for p in range(PART):
                        sp.dma_start(stack[32 * p:32 * p + 32, :, :], scratch[halves[p], :, :].rearrange("(j r) t -> r j t", j=PART))\
                            .then_inc(stacked, 16)

                def group(n, par, first, last_group):
                    restack(n, q_part, q_split, C.q_scratch, q_spilled, q_stack, q_stacked, (0, 0, 1, 1), (q_blocked, PART * n))
                    restack(n, k_part, k_split, C.k_scratch, k_spilled, k_stack[par], k_stacked, (0, 1, 0, 1),
                            (shifted, 16 * (n - 1)))

                over_groups(sp, group)



def experts(nc, C, A):
    with Phase(nc, "moe") as ph:
        w2 = ph.sb("w2", [P, E, FC, D])
        xn = ph.sb("xn", [P, GB, D])
        xnT = [ph.sb(f"xnT{i}", [P, GT]) for i in range(2)]
        x_part = [ph.sb(f"x_part{i}", [P, 2, GT], F16) for i in range(2)]
        w1_part = ph.sb("w1_part", [P, E, 2, FC, P], F16)
        w2_part = ph.sb("w2_part", [P, E, 2, FC, D], F16)
        hid = [ph.sb(f"hid{i}", [P, FC, GT]) for i in range(2)]
        h_part = [ph.sb(f"h_part{i}", [P, 2, FC, GT], F16) for i in range(2)]
        most = ph.sb("most", [P, GB])
        prob = ph.sb("prob", [P, GB, E])
        total = ph.sb("total", [P, GB])
        above = ph.sb("above", [P, GB, E, E])
        rank = ph.sb("rank", [P, GB, E])
        weight = [ph.sb(f"weight{i}", [P, GB, E]) for i in range(2)]
        H, Y, PREP, LOGITS = C.bank[0:4], C.bank[4:6], C.bank[6], C.bank[7]
        ns = norm_sems(ph)
        (w2_in, xn_ready, xnT_psum, xnT_ready, logits_ready, less_most, exps, weights_ready, hidden, silus, y_ready, added,
         route_step, zeroed, w1_hi, w1_split, w2_hi, w2_split, x_split, h_hi, h_split) = (ph.sem(n) for n in (
             "w2_in", "xn_ready", "xnT_psum", "xnT_ready", "logits_ready", "less_most", "exps", "weights_ready", "hidden",
             "silus", "y_ready", "added", "route_step", "zeroed", "w1_hi", "w1_split", "w2_hi", "w2_split", "x_split", "h_hi",
             "h_split"))
        STEPS = 2 * E + 4

        with nc.Block() as block:

            @block.sync
            def _(sp):
                for e in range(E):
                    sp.dma_start(w2[:, e, :, :], A["w2"][:, e, :, :]).then_inc(w2_in, 16)

            @block.tensor
            def _(pe):
                t = nc.tensor

                def prepare(n, step, par):
                    if step == 0:
                        pe.wait_ge(xn_ready, n + 1)
                        wait(pe, xnT_ready, n)
                        for b in range(GB):
                            last = t.transpose(PREP[:, b * P:(b + 1) * P], xn[:, b, :], C.ident[:])
                        last.then_inc(xnT_psum, 1)
                    else:
                        pe.wait_ge(xnT_ready, n + 1)
                        wait(pe, less_most, n)
                        for b in range(GB):
                            last = t.matmul(LOGITS[:, b * E:(b + 1) * E], xnT[par][:, b * P:(b + 1) * P], C.w("choice"),
                                            start=True, stop=True)
                        last.then_inc(logits_ready, 1)

                def first(n, e, c, par):
                    q = n * E + e
                    if e == 0 and c == 0:
                        pe.wait_ge(x_split, n + 1)
                    wait(pe, silus, 4 * (q - 1) + c + 1)
                    for k, (w, x) in enumerate(((0, 0), (0, 1), (1, 0))):
                        last = t.matmul(H[c][:, :], w1_part[:, e, w, c, :], x_part[par][:, x, :], start=k == 0, stop=k == 2)
                    last.then_inc(hidden, 1)

                def second(n, e, b):
                    q = n * E + e
                    if b == 0:
                        pe.wait_ge(h_split, 2 * q + 2)
                        wait(pe, added, q - 1)
                    for c in range(FC):
                        for k, (h, w) in enumerate(((0, 0), (0, 1), (1, 0))):
                            last = t.matmul(Y[e % 2][:, b * D:(b + 1) * D], h_part[e % 2][:, h, c, b * P:(b + 1) * P],
                                            w2_part[:, e, w, c, :], start=c == 0 and k == 0, stop=c == FC - 1 and k == 2)
                    if b == GB - 1:
                        last.then_inc(y_ready, 1)

                prepare(0, 0, 0)
                prepare(0, 1, 0)
                pe.wait_ge(w1_split, 1)
                for c in range(FC):
                    first(0, 0, c, 0)

                def group(n, par, is_first, is_last):
                    for e in range(E):
                        def ahead(c):
                            if e + 1 < E:
                                first(n, e + 1, c, par)
                            elif not is_last:
                                first(n + 1, 0, c, 1 - par)

                        if is_first and e + 1 < E:
                            pe.wait_ge(w1_split, e + 2)
                        for c in range(FC):
                            ahead(c)
                        if is_first:
                            pe.wait_ge(w2_split, e + 1)
                        for b in range(GB):
                            second(n, e, b)
                            if b == 1 and e < 2 and not is_last:
                                prepare(n + 1, e, 1 - par)

                over_groups(pe, group)

            @block.scalar
            def _(act):
                a = nc.scalar

                def transposed(n, par):
                    act.wait_ge(xnT_psum, n + 1)
                    wait(act, logits_ready, n - 1)
                    wait(act, x_split, n - 1)
                    wait(act, hidden, 32 * (n - 1))
                    a.activation(x_part[par][:, 0, :], PREP[:, :], ACT.Copy, scale=X_LIFT)
                    a.activation(xnT[par][:], PREP[:, :], ACT.Copy).then_inc(xnT_ready, 1)

                def exponential(n):
                    act.wait_ge(less_most, n + 1)
                    a.activation(prob[:], prob[:], ACT.Exp).then_inc(exps, 1)

                def silu(n, e, c):
                    q = n * E + e
                    act.wait_ge(hidden, 4 * q + c + 1)
                    if c == 0:
                        wait(act, h_split, 2 * (q - 1))
                    a.activation(hid[e % 2][:, c, :], H[c][:, :], ACT.Silu, scale=1.0 / (X_LIFT * W_LIFT)).then_inc(silus, 1)

                def high(n, e, half):
                    q = n * E + e
                    if half == 0:
                        wait(act, y_ready, q - 1)
                    act.wait_ge(silus, 4 * q + 2 * half + 2)
                    c = slice(2 * half, 2 * half + 2)
                    a.activation(h_part[e % 2][:, 0, c, :], hid[e % 2][:, c, :], ACT.Copy, scale=H_LIFT).then_inc(h_hi, 1)

                def hidden_values(n, e):
                    for c in range(3):
                        silu(n, e, c)
                    high(n, e, 0)
                    silu(n, e, 3)
                    high(n, e, 1)

                norm_root(nc, C, act, ns)
                act.wait_ge(C.w1_in, 16)
                for e in range(E):
                    a.activation(w1_part[:, e, 0, :, :], C.w1[:, e, :, :], ACT.Copy, scale=W_LIFT).then_inc(w1_hi, 1)
                transposed(0, 0)
                exponential(0)
                hidden_values(0, 0)
                act.wait_ge(w2_in, 16 * E)
                for e in range(E):
                    a.activation(w2_part[:, e, 0, :, :], w2[:, e, :, :], ACT.Copy, scale=W_LIFT).then_inc(w2_hi, 1)

                def group(n, par, is_first, is_last):
                    for e in range(E):
                        if e + 1 < E:
                            hidden_values(n, e + 1)
                        elif not is_last:
                            hidden_values(n + 1, 0)
                        if e == 0 and not is_last:
                            transposed(n + 1, 1 - par)
                        if e == 2 and not is_last:
                            exponential(n + 1)

                over_groups(act, group)

            @block.vector
            def _(dve):
                v = nc.vector
                norm_vector(nc, C, dve, ns)

                def layer_norm(n):
                    wait(dve, xnT_psum, n)
                    normalized(nc, C, xn, n).then_inc(xn_ready, 1)

                def less_maximum(n):
                    dve.wait_ge(logits_ready, n + 1)
                    wait(dve, route_step, STEPS * n)
                    lg = LOGITS[:, 0:GB * E].rearrange("p (b e) -> p b e", b=GB)
                    v.tensor_reduce(most[:], lg, AX.X, ALU.max).then_inc(route_step, 1)
                    dve.wait_ge(route_step, STEPS * n + 1)
                    v.tensor_tensor(prob[:], lg, most[:].unsqueeze(2).to_broadcast([P, GB, E]), ALU.subtract)\
                        .then_inc(less_most, 1)

                def softmax(n):
                    base = STEPS * n + 1
                    dve.wait_ge(exps, n + 1)
                    v.tensor_reduce(total[:], prob[:], AX.X, ALU.add).then_inc(route_step, 1)
                    dve.wait_ge(route_step, base + 1)
                    v.reciprocal(total[:], total[:]).then_inc(route_step, 1)
                    dve.wait_ge(route_step, base + 2)
                    v.tensor_tensor(prob[:], prob[:], total[:].unsqueeze(2).to_broadcast([P, GB, E]), ALU.mult)\
                        .then_inc(route_step, 1)

                def rank_experts(n, par):
                    base = STEPS * n + 1
                    dve.wait_ge(route_step, base + 3)
                    for e in range(E):
                        if e + 1 < E:
                            v.tensor_tensor(above[:, :, e, e + 1:], prob[:, :, e:e + 1].to_broadcast([P, GB, E - 1 - e]),
                                            prob[:, :, e + 1:], ALU.is_ge).then_inc(route_step, 1)
                        if e:
                            v.tensor_tensor(above[:, :, e, 0:e], prob[:, :, e:e + 1].to_broadcast([P, GB, e]),
                                            prob[:, :, 0:e], ALU.is_gt).then_inc(route_step, 1)
                    dve.wait_ge(route_step, base + 3 + 2 * E - 2)
                    v.tensor_reduce(rank[:], above[:].rearrange("p b f e -> p b e f"), AX.X, ALU.add).then_inc(route_step, 1)
                    dve.wait_ge(route_step, base + 2 + 2 * E)
                    v.tensor_scalar(rank[:], rank[:], 1.5, 1.0 / (H_LIFT * W_LIFT), ALU.is_lt, ALU.mult).then_inc(route_step, 1)
                    dve.wait_ge(route_step, base + 3 + 2 * E)
                    v.tensor_tensor(weight[par][:], rank[:], prob[:], ALU.mult).then_inc(weights_ready, 1)

                def low(out, full, lift, hi):
                    return v.scalar_tensor_tensor(out=out, in0=full, scalar=lift, in1=hi, op0=ALU.mult, op1=ALU.subtract)

                def split_tokens(n, par):
                    dve.wait_ge(xnT_ready, n + 1)
                    low(x_part[par][:, 1, :], xnT[par][:], X_LIFT, x_part[par][:, 0, :]).then_inc(x_split, 1)

                def split_hidden(n, e):
                    for half in range(2):
                        dve.wait_ge(h_hi, 2 * (n * E + e) + half + 1)
                        c = slice(2 * half, 2 * half + 2)
                        low(h_part[e % 2][:, 1, c, :], hid[e % 2][:, c, :], H_LIFT, h_part[e % 2][:, 0, c, :]).then_inc(h_split, 1)

                def add(n, e, par):
                    q = n * E + e
                    dve.wait_ge(y_ready, q + 1)
                    if e == 0:
                        dve.wait_ge(weights_ready, n + 1)
                    else:
                        dve.wait_ge(added, q)
                    for b in range(GB):
                        xb = C.x[:, batch(n, b), :]
                        last = v.scalar_tensor_tensor(out=xb, in0=Y[e % 2][:, b * D:(b + 1) * D].unsqueeze(1),
                                                      scalar=weight[par][:, b, e:e + 1], in1=xb, op0=ALU.mult, op1=ALU.add)
                    last.then_inc(added, 1)

                layer_norm(0)
                v.memset(above[:], 0.0).then_inc(zeroed, 1)
                dve.wait_ge(zeroed, 1)
                for e in range(E):
                    dve.wait_ge(w1_hi, e + 1)
                    low(w1_part[:, e, 1, :, :], C.w1[:, e, :, :], W_LIFT, w1_part[:, e, 0, :, :]).then_inc(w1_split, 1)
                    if e == 0:
                        split_tokens(0, 0)
                less_maximum(0)
                softmax(0)
                rank_experts(0, 0)
                split_hidden(0, 0)
                for e in range(E):
                    dve.wait_ge(w2_hi, e + 1)
                    low(w2_part[:, e, 1, :, :], w2[:, e, :, :], W_LIFT, w2_part[:, e, 0, :, :]).then_inc(w2_split, 1)

                def group(n, par, is_first, is_last):
                    if not is_last:
                        layer_norm(n + 1)
                    for e in range(E):
                        if e + 1 < E:
                            split_hidden(n, e + 1)
                        elif not is_last:
                            split_hidden(n + 1, 0)
                        if e == 0 and not is_last:
                            split_tokens(n + 1, 1 - par)
                        add(n, e, par)
                        if e == 2 and not is_last:
                            less_maximum(n + 1)
                        if e == 3 and not is_last:
                            softmax(n + 1)
                        if e == 5 and not is_last:
                            rank_experts(n + 1, 1 - par)
                    dve.wait_ge(added, n * E + E)
                    for b in range(GB):
                        v.bn_stats(C.stats[:, batch(n, b), :], C.x[:, batch(n, b), :])

                over_groups(dve, group)
                v.engine_nop().then_inc(zeroed, 1)
                dve.wait_ge(zeroed, 2)



def quantized_gated(nc, C):
    with nc.sbuf_tensor("gated", [P, 3, NB * P], F32) as h:
        with Phase(nc, "qmax") as ph:
            ends = ph.sb("ends", [P, 2, NB])
            ns = norm_sems(ph)
            end_step, step, peak_ready, peak_all, clip_ready = (
                ph.sem(n) for n in ("end_step", "step", "peak_ready", "peak_all", "clip_ready"))
            with nc.Block() as block:

                @block.vector
                def _(dve):
                    v = nc.vector
                    ch = Chain(dve, end_step)
                    ch(v.tensor_reduce(ends[:, 0, :], C.x[:], AX.X, ALU.max))
                    ch(v.tensor_reduce(ends[:, 1, :], C.x[:], AX.X, ALU.min))
                    norm_vector(nc, C, dve, ns)
                    ch(v.tensor_tensor(ends[:], ends[:], C.rstd[:].unsqueeze(1).to_broadcast([P, 2, NB]), ALU.mult))
                    ch(v.tensor_tensor(ends[:], ends[:], C.shift[:].unsqueeze(1).to_broadcast([P, 2, NB]), ALU.add))
                    v.tensor_reduce(C.peak[:, 0:1], ends[:], AX.XY, ALU.max, apply_absolute_value=True).then_inc(peak_ready, 1)
                    dve.wait_ge(peak_all, 1)
                    dve.wait_ge(clip_ready, 1)
                    activation_scale(nc, C, dve, step, 0)

                @block.gpsimd
                def _(pool):
                    all_peak(nc, C, pool, peak_ready, peak_all, 0)

                @block.scalar
                def _(act):
                    norm_root(nc, C, act, ns)
                    c = ROWS["clip_x"][0]
                    nc.scalar.activation(C.clip[:], C.rows[:, c:c + 2], ACT.Sigmoid).then_inc(clip_ready, 1)

        with Phase(nc, "qup") as ph:
            xn = [ph.sb(f"xn{i}", [P, GB, D]) for i in range(2)]
            xi = [ph.sb(f"xi{i}", [P, GB, D]) for i in range(2)]
            xqT = [ph.sb(f"xqT{i}", [P, GT], BF16) for i in range(2)]
            gate = ph.sb("gate", [P, 3, GT])
            scales = ph.sb("scales", [P, 6])
            peaks = ph.sb("peaks", [P, NG])
            unmagic = ph.sb("unmagic", [P, 1])
            (xn_ready, rounded, xi_ready, xT_psum, xq_ready, gates, ups, silus, h_ready, peak_read, step, peak_ready,
             peak_all, scales_ready, const_ready) = (ph.sem(n) for n in (
                 "xn_ready", "rounded", "xi_ready", "xT_psum", "xq_ready", "gates", "ups", "silus", "h_ready", "peak_read",
                 "step", "peak_ready", "peak_all", "scales_ready", "const_ready"))
            G, U, PREP = C.bank[0:3], C.bank[3:6], C.bank[6:8]
            with nc.Block() as block:

                @block.vector
                def _(dve):
                    v = nc.vector
                    v.tensor_scalar(scales[:], C.wscale[:, 0:6], C.scale[:, 0:1], None, ALU.mult).then_inc(scales_ready, 1)
                    dve.wait_ge(scales_ready, 1)

                    def layer_norm(n, par):
                        wait(dve, rounded, n - 1)
                        normalized(nc, C, xn[par], n).then_inc(xn_ready, 1)

                    layer_norm(0, 0)
                    layer_norm(1, 1)

                    def group(n, par, first, last_group):
                        if not (isinstance(n, int) and n + 2 >= NG):
                            layer_norm(n + 2, par)
                        for c in range(3):
                            dve.wait_ge(silus, 3 * n + c + 1)
                            dve.wait_ge(ups, 3 * n + c + 1)
                            v.scalar_tensor_tensor(out=h[:, c, bass.ds(n * GT, GT)], in0=U[c][:, :], scalar=scales[:, 3 + c:4 + c],
                                                   in1=gate[:, c, :], op0=ALU.mult, op1=ALU.mult).then_inc(h_ready, 1)
                        dve.wait_ge(h_ready, 3 * n + 3)
                        v.tensor_reduce(peaks[:, bass.ds(n, 1)], h[:, :, bass.ds(n * GT, GT)], AX.XY, ALU.max,
                                        apply_absolute_value=True).then_inc(peak_read, 1)

                    over_groups(dve, group)
                    dve.wait_ge(peak_read, NG)
                    v.tensor_reduce(C.peak[:, 1:2], peaks[:], AX.X, ALU.max).then_inc(peak_ready, 1)
                    dve.wait_ge(peak_all, 1)
                    activation_scale(nc, C, dve, step, 1)

                @block.gpsimd
                def _(pool):
                    g = nc.gpsimd
                    g.memset(unmagic[:], -MAGIC).then_inc(const_ready, 1)

                    def group(n, par, first, last_group):
                        round_clipped(C, pool, xi[par][:], xn[par][:], C.scale[:, 2:3], xn_ready, n, (xT_psum, n - 1), rounded,
                                      xi_ready, g)

                    over_groups(pool, group)
                    all_peak(nc, C, pool, peak_ready, peak_all, 1)

                @block.scalar
                def _(act):
                    a = nc.scalar
                    act.wait_ge(const_ready, 1)

                    def integers(n, par):
                        act.wait_ge(xT_psum, n + 1)
                        wait(act, ups, 3 * (n - 1))
                        a.activation(xqT[par][:], PREP[par][:, :], ACT.Identity, bias=unmagic[:]).then_inc(xq_ready, 1)

                    integers(0, 0)
                    act.wait_ge(scales_ready, 1)

                    def group(n, par, first, last_group):
                        if not last_group:
                            integers(n + 1, 1 - par)
                        for c in range(3):
                            act.wait_ge(gates, 3 * n + c + 1)
                            wait(act, h_ready, 3 * (n - 1) + c + 1)
                            a.activation(gate[:, c, :], G[c][:, :], ACT.Silu, scale=scales[:, c:c + 1]).then_inc(silus, 1)

                    over_groups(act, group)

                @block.tensor
                def _(pe):
                    t = nc.tensor

                    def turn(n, par):
                        pe.wait_ge(xi_ready, n + 1)
                        wait(pe, xq_ready, n - 1)
                        for b in range(GB):
                            last = t.transpose(PREP[par][:, b * P:(b + 1) * P], xi[par][:, b, :], C.ident[:])
                        last.then_inc(xT_psum, 1)

                    turn(0, 0)

                    def group(n, par, first, last_group):
                        if not last_group:
                            turn(n + 1, 1 - par)
                        pe.wait_ge(xq_ready, n + 1)
                        for c in range(3):
                            wait(pe, silus, 3 * (n - 1) + c + 1)
                            t.matmul(G[c][:, :], C.wquant[:, c, :], xqT[par][:], start=True, stop=True).then_inc(gates, 1)
                            wait(pe, h_ready, 3 * (n - 1) + c + 1)
                            t.matmul(U[c][:, :], C.wquant[:, 3 + c, :], xqT[par][:], start=True, stop=True).then_inc(ups, 1)

                    over_groups(pe, group)

        with Phase(nc, "qdown") as ph:
            hq = [ph.sb(f"hq{i}", [P, 3, GT], BF16) for i in range(2)]
            out = [ph.sb(f"out{i}", [P, GB, D]) for i in range(2)]
            col_scale = ph.sb("col_scale", [P, D])
            unmagic = ph.sb("unmagic", [P, 1])
            magic = ph.sb("magic", [P, 1])
            (rounded, hi_ready, hq_ready, downs, scaled, added, col_ready, const_ready) = (ph.sem(n) for n in (
                "rounded", "hi_ready", "hq_ready", "downs", "scaled", "added", "col_ready", "const_ready"))
            Y = C.bank[0:2]
            with nc.Block() as block:

                @block.gpsimd
                def _(pool):
                    nc.gpsimd.memset(magic[:], MAGIC)
                    nc.gpsimd.memset(unmagic[:], -MAGIC).then_inc(const_ready, 1)

                    def group(n, par, first, last_group):
                        pool.wait_ge(scaled, n + 1)
                        xg = C.x[:, batch(n, 0, GB), :]
                        nc.gpsimd.tensor_tensor(xg, xg, out[par][:], ALU.add).then_inc(added, 1)

                    over_groups(pool, group)

                @block.scalar
                def _(act):
                    act.wait_ge(const_ready, 1)

                    def rounds(n):
                        part = h[:, :, bass.ds(n * GT, GT)]
                        nc.scalar.activation(part, part, ACT.Identity, scale=C.scale[:, 3:4], bias=magic[:]).then_inc(rounded, 1)

                    rounds(0)

                    def group(n, par, first, last_group):
                        if not last_group:
                            rounds(n + 1)
                        act.wait_ge(hi_ready, n + 1)
                        wait(act, downs, n - 1)
                        apart(act, C)
                        nc.scalar.activation(hq[par][:], h[:, :, bass.ds(n * GT, GT)], ACT.Identity, bias=unmagic[:]).then_inc(hq_ready, 1)

                    over_groups(act, group)

                @block.tensor
                def _(pe):
                    def group(n, par, first, last_group):
                        pe.wait_ge(hq_ready, n + 1)
                        wait(pe, scaled, n - 1)
                        for b in range(GB):
                            for c in range(3):
                                last = nc.tensor.matmul(Y[par][:, b * D:(b + 1) * D], hq[par][:, c, b * P:(b + 1) * P],
                                                        C.wquant[:, 6 + c, :], start=c == 0, stop=c == 2)
                        last.then_inc(downs, 1)

                    over_groups(pe, group)

                @block.vector
                def _(dve):
                    v = nc.vector
                    v.tensor_scalar(col_scale[:], C.down_scale[:], C.scale[:, 1:2], None, ALU.mult).then_inc(col_ready, 1)
                    dve.wait_ge(col_ready, 1)

                    def clip(n):
                        part = h[:, :, bass.ds(n * GT, GT)]
                        dve.wait_ge(rounded, n + 1)
                        v.tensor_scalar(part, part, MAGIC + QMAX, MAGIC - QMAX - 1.0, ALU.min, ALU.max).then_inc(hi_ready, 1)

                    def statistics(n):
                        dve.wait_ge(added, n + 1)
                        for b in range(GB):
                            v.bn_stats(C.stats[:, batch(n, b), :], C.x[:, batch(n, b), :])

                    clip(0)

                    def group(n, par, first, last_group):
                        if not last_group:
                            clip(n + 1)
                        dve.wait_ge(downs, n + 1)
                        wait(dve, added, n - 1)
                        v.tensor_tensor(out[par][:], Y[par][:, :].rearrange("p (b d) -> p b d", b=GB),
                                        col_scale[:].unsqueeze(1).to_broadcast([P, GB, D]), ALU.mult).then_inc(scaled, 1)
                        if not first:
                            statistics(n - 1)

                    over_groups(dve, group)
                    statistics(NG - 1)
                    v.engine_nop().then_inc(col_ready, 1)
                    dve.wait_ge(col_ready, 2)


def activation_scale(nc, C, dve, step, k):
    ch = Chain(dve, step)
    ch(nc.vector.tensor_scalar(C.scale[:, k:k + 1], C.peak[:, 2 + k:3 + k], C.clip[:, k:k + 1], 1.0 / QMAX, ALU.mult, ALU.mult))
    ch(nc.vector.reciprocal(C.scale[:, 2 + k:3 + k], C.scale[:, k:k + 1]))


def all_peak(nc, C, pool, ready, done, k):
    pool.wait_ge(ready, 1)
    nc.gpsimd.partition_all_reduce(C.peak[:, 2 + k:3 + k], C.peak[:, k:k + 1], P, bass.bass_isa.ReduceOp.max).then_inc(done, 1)


def round_clipped(C, pool, out, x, inv, ready, n, free, rounded, done, g):
    if ready is not None:
        pool.wait_ge(ready, n + 1)
    wait(pool, *free)
    apart(pool, C)
    g.tensor_scalar(out, x, inv, MAGIC, ALU.mult, ALU.add).then_inc(rounded, 1)
    pool.wait_ge(rounded, n + 1)
    apart(pool, C)
    g.tensor_scalar(out, out, MAGIC + QMAX, MAGIC - QMAX - 1.0, ALU.min, ALU.max).then_inc(done, 1)



def tree(nc, C):
    with Phase(nc, "tree") as ph:
        xn = ph.sb("xn", [P, GB, D])
        xnT = [ph.sb(f"xnT{i}", [P, GT]) for i in range(2)]
        right = [ph.sb(f"right{i}", [P, GB, LEAVES]) for i in range(2)]
        left = [ph.sb(f"left{i}", [P, GB, LEAVES]) for i in range(2)]
        level = [ph.sb(f"level{i}", [P, GB, LEAVES // 2]) for i in range(2)]
        leaf = [ph.sb(f"leaf{i}", [P, GB, LEAVES]) for i in range(2)]
        leafT = ph.sb("leafT", [P, 2, GT])
        x_bias = [ph.sb(f"x_bias{i}", [P, GB, D]) for i in range(2)]
        PREP, G, LT, OUT = C.bank[0], C.bank[1:3], C.bank[3:5], C.bank[5:7]
        ns = norm_sems(ph)
        (xn_ready, xnT_psum, xnT_ready, gates, rights, lefts, step, left_leaves, right_leaves, leafT_psum, leafT_ready, outs, added, xb_ready, end) = (
            ph.sem(n) for n in ("xn_ready", "xnT_psum", "xnT_ready", "gates", "rights", "lefts", "step", "left_leaves",
                                "right_leaves", "leafT_psum", "leafT_ready", "outs", "added", "xb_ready", "end"))
        DEPTH = 8
        STEPS = 2 * (DEPTH - 1)
        with nc.Block() as block:

            @block.tensor
            def _(pe):
                t = nc.tensor

                def turn(n, par):
                    pe.wait_ge(xn_ready, n + 1)
                    wait(pe, xnT_ready, n)
                    for b in range(GB):
                        last = t.transpose(PREP[:, b * P:(b + 1) * P], xn[:, b, :], C.ident[:])
                    last.then_inc(xnT_psum, 1)

                def route(n, par):
                    pe.wait_ge(xnT_ready, n + 1)
                    for k in range(2):
                        wait(pe, rights, 2 * (n - 1) + k + 1)
                        for b in range(2):
                            last = t.matmul(G[k][:, b * LEAVES:(b + 1) * LEAVES], xnT[par][:, (2 * k + b) * P:(2 * k + b + 1) * P],
                                            C.route[:], start=True, stop=True)
                        last.then_inc(gates, 1)

                turn(0, 0)
                turn(1, 1)
                route(0, 0)

                def group(n, par, first, last_group):
                    if not last_group:
                        route(n + 1, 1 - par)
                    pe.wait_ge(left_leaves, n + 1)
                    pe.wait_ge(right_leaves, n + 1)
                    for c in range(2):
                        wait(pe, leafT_ready, 2 * (n - 1) + c + 1)
                        for b in range(GB):
                            last = t.transpose(LT[c][:, b * P:(b + 1) * P], leaf[par][:, b, c * P:(c + 1) * P], C.ident[:])
                        last.then_inc(leafT_psum, 1)
                    if not (isinstance(n, int) and n + 2 >= NG):
                        turn(n + 2, par)
                    pe.wait_ge(leafT_ready, 2 * n + 2)
                    wait(pe, added, n - 1)
                    for b in range(GB):
                        for c in range(2):
                            last = t.matmul(OUT[par][:, b * D:(b + 1) * D], leafT[:, c, b * P:(b + 1) * P], C.leaf[:, c, :],
                                            start=c == 0, stop=c == 1)
                    last.then_inc(outs, 1)

                over_groups(pe, group)

            @block.scalar
            def _(act):
                a = nc.scalar

                def layer_norm(n):
                    wait(act, xnT_psum, n)
                    apart(act, C)
                    for b in range(GB):
                        last = a.activation(xn[:, b:b + 1, :], C.x[:, batch(n, b), :], ACT.Identity, scale=C.rstd[:, batch(n, b)],
                                            bias=C.shift[:, batch(n, b)])
                    last.then_inc(xn_ready, 1)

                def transposed(n, par):
                    act.wait_ge(xnT_psum, n + 1)
                    wait(act, gates, 2 * (n - 1))
                    a.activation(xnT[par][:], PREP[:, :], ACT.Copy).then_inc(xnT_ready, 1)

                def sigmoids(n, par):
                    wait(act, left_leaves, n - 1)
                    wait(act, right_leaves, n - 1)
                    for k in range(2):
                        act.wait_ge(gates, 2 * n + k + 1)
                        a.activation(right[par][:, 2 * k:2 * k + 2, :], G[k][:, :].rearrange("p (b m) -> p b m", b=2), ACT.Sigmoid)\
                            .then_inc(rights, 1)

                norm_root(nc, C, act, ns)
                act.wait_ge(ns["norm_step"], NORM_STEPS)
                layer_norm(0)
                transposed(0, 0)
                layer_norm(1)
                transposed(1, 1)
                sigmoids(0, 0)

                def group(n, par, first, last_group):
                    more = not (isinstance(n, int) and n + 2 >= NG)
                    if more:
                        layer_norm(n + 2)
                    if not last_group:
                        sigmoids(n + 1, 1 - par)
                    wait(act, outs, n)
                    for c in range(2):
                        act.wait_ge(leafT_psum, 2 * n + c + 1)
                        a.activation(leafT[:, c, :], LT[c][:, :], ACT.Copy).then_inc(leafT_ready, 1)
                    if more:
                        transposed(n + 2, par)

                over_groups(act, group)

            @block.vector
            def _(dve):
                v = nc.vector
                norm_vector(nc, C, dve, ns)

                def add(n, par):
                    dve.wait_ge(outs, n + 1)
                    dve.wait_ge(xb_ready, n + 1)
                    v.tensor_tensor(C.x[:, batch(n, 0, GB), :], OUT[par][:, :].rearrange("p (b d) -> p b d", b=GB),
                                    x_bias[par][:], ALU.add).then_inc(added, 1)
                    dve.wait_ge(added, n + 1)
                    for b in range(GB):
                        v.bn_stats(C.stats[:, batch(n, b), :], C.x[:, batch(n, b), :])

                def descend(n, par):
                    dve.wait_ge(rights, 2 * n + 2)
                    dve.wait_ge(lefts, n + 1)
                    base = STEPS * n
                    wait(dve, step, base)
                    wait(dve, left_leaves, n)
                    wait(dve, right_leaves, n)
                    l, r = left[par], right[par]
                    v.tensor_copy(level[0][:, :, 0:1], l[:, :, 0:1]).then_inc(step, 1)
                    v.tensor_copy(level[0][:, :, 1:2], r[:, :, 0:1]).then_inc(step, 1)
                    for k in range(1, DEPTH - 1):
                        dve.wait_ge(step, base + 2 * k)
                        for side, gate in enumerate((l, r)):
                            v.tensor_tensor(children(level[k % 2], k, side), level[(k - 1) % 2][:, :, 0:2 ** k],
                                            at_level(gate, k), ALU.mult).then_inc(step, 1)
                    dve.wait_ge(step, base + STEPS)
                    wait(dve, leafT_psum, 2 * (n - 1))
                    v.tensor_tensor(children(leaf[par], DEPTH - 1, 0), level[DEPTH % 2][:, :, :], at_level(l, DEPTH - 1),
                                    ALU.mult).then_inc(left_leaves, 1)

                def group(n, par, first, last_group):
                    descend(n, par)
                    if not first:
                        add(n - 1, 1 - par)

                over_groups(dve, group)
                add(NG - 1, (NG - 1) % 2)
                v.engine_nop().then_inc(end, 1)
                dve.wait_ge(end, 1)

            @block.gpsimd
            def _(pool):
                g = nc.gpsimd

                def turn_left(n, par):
                    pool.wait_ge(rights, 2 * n + 2)
                    wait(pool, left_leaves, n - 1)
                    apart(pool, C)
                    g.tensor_scalar(left[par][:], right[par][:], -1.0, 1.0, ALU.mult, ALU.add).then_inc(lefts, 1)

                def bias(n, par):
                    wait(pool, added, n - 1)
                    g.tensor_tensor(x_bias[par][:], C.x[:, batch(n, 0, GB), :], C.row("tree_b").unsqueeze(1).to_broadcast([P, GB, D]),
                                    ALU.add).then_inc(xb_ready, 1)

                def last_rights(n, par):
                    pool.wait_ge(step, STEPS * (n + 1))
                    wait(pool, leafT_psum, 2 * (n - 1))
                    g.tensor_tensor(children(leaf[par], DEPTH - 1, 1), level[DEPTH % 2][:, :, :], at_level(right[par], DEPTH - 1),
                                    ALU.mult).then_inc(right_leaves, 1)

                turn_left(0, 0)

                def group(n, par, first, last_group):
                    last_rights(n, par)
                    if not last_group:
                        turn_left(n + 1, 1 - par)
                    bias(n, par)

                over_groups(pool, group)


def children(nodes, k, side):
    return nodes[:, :, 0:2 ** (k + 1)].rearrange("p b (m s) -> p b m s", s=2)[:, :, :, side]


def at_level(gate, k):
    return gate[:, :, 2 ** k - 1:2 ** (k + 1) - 1]



def channel_mix(nc, C, A):
    with Phase(nc, "mix") as ph:
        xn = ph.sb("xn", [P, GB, D])
        xT = [ph.sb(f"xT{i}", [P, GB, P + 1]) for i in range(2)]
        step_back = ph.sb("step_back", [P, GB, P])
        xr = [ph.sb(f"xr{i}", [P, GB, P]) for i in range(2)]
        xk = [ph.sb(f"xk{i}", [P, GB, P]) for i in range(2)]
        relu = ph.sb("relu", [P, GT])
        kact = ph.sb("kact", [P, GT])
        gate = [ph.sb(f"gate{i}", [P, GB, D]) for i in range(2)]
        out = [ph.sb(f"out{i}", [P, GB, D]) for i in range(2)]
        PREP, R, K, V = C.bank[0], C.bank[1:3], C.bank[3:5], C.bank[5:7]
        ns = norm_sems(ph)
        (zeroed, xn_ready, xT_psum, xT_ready, back_ready, mixed, r_psum, k_psum, v_psum, relus, squares, gates, products,
         finals, stored) = (ph.sem(n) for n in (
             "zeroed", "xn_ready", "xT_psum", "xT_ready", "back_ready", "mixed", "r_psum", "k_psum", "v_psum", "relus",
             "squares", "gates", "products", "finals", "stored"))
        with nc.Block() as block:

            @block.tensor
            def _(pe):
                t = nc.tensor

                def turn(n):
                    pe.wait_ge(xn_ready, n + 1)
                    wait(pe, xT_ready, n)
                    for b in range(GB):
                        last = t.transpose(PREP[:, b * P:(b + 1) * P], xn[:, b, :], C.ident[:])
                    last.then_inc(xT_psum, 1)

                turn(0)
                turn(1)

                def group(n, par, first, last_group):
                    pe.wait_ge(mixed, 2 * n + 2)
                    wait(pe, relus, n - 1)
                    t.matmul(K[par][:, :], C.w("mix_k"), xk[par][:].rearrange("p b t -> p (b t)"), start=True, stop=True)\
                        .then_inc(k_psum, 1)
                    wait(pe, gates, n - 1)
                    for b in range(GB):
                        last = t.matmul(R[par][:, b * D:(b + 1) * D], xr[par][:, b, :], C.w("mix_r"), start=True, stop=True)
                    last.then_inc(r_psum, 1)
                    if not (isinstance(n, int) and n + 2 >= NG):
                        turn(n + 2)
                    pe.wait_ge(squares, n + 1)
                    wait(pe, products, n - 1)
                    for b in range(GB):
                        last = t.matmul(V[par][:, b * D:(b + 1) * D], kact[:, b * P:(b + 1) * P], C.w("mix_v"), start=True, stop=True)
                    last.then_inc(v_psum, 1)

                over_groups(pe, group)

            @block.scalar
            def _(act):
                a = nc.scalar
                norm_root(nc, C, act, ns)
                act.wait_ge(zeroed, 2)

                def transposed(n, par):
                    act.wait_ge(xT_psum, n + 1)
                    wait(act, mixed, 2 * (n - 1))
                    a.activation(xT[par][:, :, 1:], PREP[:, :].rearrange("p (b t) -> p b t", b=GB), ACT.Copy).then_inc(xT_ready, 1)

                transposed(0, 0)
                transposed(1, 1)

                def group(n, par, first, last_group):
                    act.wait_ge(k_psum, n + 1)
                    wait(act, squares, n)
                    a.activation(relu[:], K[par][:, :], ACT.Relu).then_inc(relus, 1)
                    act.wait_ge(r_psum, n + 1)
                    wait(act, products, n - 1)
                    a.activation(gate[par][:], R[par][:, :].rearrange("p (b d) -> p b d", b=GB), ACT.Sigmoid).then_inc(gates, 1)
                    if not (isinstance(n, int) and n + 2 >= NG):
                        transposed(n + 2, par)

                over_groups(act, group)

            @block.vector
            def _(dve):
                v = nc.vector
                for i in range(2):
                    v.memset(xT[i][:, :, 0:1], 0.0).then_inc(zeroed, 1)
                norm_vector(nc, C, dve, ns)

                def layer_norm(n):
                    wait(dve, xT_psum, n)
                    normalized(nc, C, xn, n).then_inc(xn_ready, 1)

                def mix(n, par):
                    dve.wait_ge(xT_ready, n + 1)
                    wait(dve, mixed, 2 * n)
                    now, before = xT[par][:, :, 1:], xT[par][:, :, 0:P]
                    v.tensor_tensor(step_back[:], now, before, ALU.subtract).then_inc(back_ready, 1)
                    dve.wait_ge(back_ready, n + 1)
                    wait(dve, v_psum, n - 1)
                    for o, mu in ((xk, "mu_k"), (xr, "mu_r")):
                        v.scalar_tensor_tensor(out=o[par][:], in0=step_back[:], scalar=C.w(mu), in1=before,
                                               op0=ALU.mult, op1=ALU.add).then_inc(mixed, 1)

                def product(n, par):
                    dve.wait_ge(v_psum, n + 1)
                    dve.wait_ge(gates, n + 1)
                    wait(dve, finals, n - 1)
                    v.tensor_tensor(out[par][:], V[par][:, :].rearrange("p (b d) -> p b d", b=GB), gate[par][:], ALU.mult)\
                        .then_inc(products, 1)

                layer_norm(0)
                layer_norm(1)
                mix(0, 0)

                def group(n, par, first, last_group):
                    if not (isinstance(n, int) and n + 2 >= NG):
                        layer_norm(n + 2)
                    if not last_group:
                        mix(n + 1, 1 - par)
                    product(n, par)

                over_groups(dve, group)

            @block.gpsimd
            def _(pool):
                g = nc.gpsimd

                def group(n, par, first, last_group):
                    pool.wait_ge(relus, n + 1)
                    wait(pool, v_psum, n)
                    g.tensor_tensor(kact[:], relu[:], relu[:], ALU.mult).then_inc(squares, 1)
                    if not first:
                        final(n - 1, 1 - par)

                def final(n, par):
                    pool.wait_ge(products, n + 1)
                    xg = C.x[:, batch(n, 0, GB), :]
                    g.tensor_tensor(xg, xg, out[par][:], ALU.add).then_inc(finals, 1)

                over_groups(pool, group)
                final(NG - 1, (NG - 1) % 2)

            @block.sync
            def _(sp):
                def group(n, par, first, last_group):
                    sp.wait_ge(finals, n + 1)
                    sp.dma_start(A["out"][:, batch(n, 0, GB), :], C.x[:, batch(n, 0, GB), :]).then_inc(stored, 16)

                over_groups(sp, group)
                sp.wait_ge(stored, 16 * NG)


def diagonal(o):
    o = o.rearrange("k g (j c) -> k g j c", c=32)
    steps = [list(x) for x in o.ap]
    steps[2] = [steps[2][0] + DH, PART]
    steps[3] = [steps[3][0], DH]
    return bass.AP(tensor=o.tensor, offset=o.offset, ap=steps)


def program(nc, A):
    with ExitStack() as stack:
        C = Chip()

        def sb(name, shape, dt=F32):
            return stack.enter_context(nc.sbuf_tensor(name, shape, dt))

        C.q_scratch = nc.dram_tensor("q_scratch", (2, P, GT), F16)
        C.k_scratch = nc.dram_tensor("k_scratch", (2, P, GK), F16)
        C.ctx_in = stack.enter_context(nc.semaphore("ctx_in"))
        C.w1_in = stack.enter_context(nc.semaphore("w1_in"))
        C.passed = stack.enter_context(nc.semaphore("passed"))
        C.bank = [stack.enter_context(nc.psum_tensor(f"bank{i}", [P, 512], F32)) for i in range(8)]
        C.x = sb("x_res", [P, NB, D])
        C.ctxT = sb("ctxT", [P, NB, TK])
        C.pack = sb("pack_sb", [P, PACK_COLS])
        C.rows = sb("rows_sb", [P, ROW_COLS])
        C.w = lambda name: C.pack[:, PACK[name][0]:PACK[name][0] + PACK[name][1]]
        C.row = lambda name: C.rows[:, ROWS[name][0]:ROWS[name][0] + ROWS[name][1]]
        C.stats = sb("stats", [P, NB, 6])
        C.norm_tmp = sb("norm_tmp", [P, 3, NB])
        C.rstd = sb("rstd", [P, NB])
        C.shift = sb("shift", [P, NB])
        C.ident = sb("ident", [P, P])
        C.neg_ident = sb("neg_ident", [P, P], BF16)
        C.neg_big = sb("neg_big", [P, P], BF16)
        C.pos_big = sb("pos_big", [P, P], BF16)
        C.head_rows = sb("head_rows", [P, PART])
        C.head_cols = sb("head_cols", [P, PART, 32])
        C.mask2 = sb("mask2", [P, TK], BF16)
        C.mask2_less = sb("mask2_less", [P, TK], BF16)
        C.lowest2 = sb("lowest2", [P, 1], BF16)
        C.lens = sb("lens", [P, NB])
        C.key_row = sb("key_row", [P, TK])
        C.keep0 = sb("keep0", [P, NB])
        C.bias0 = sb("bias0", [P, NB])
        C.wquant = sb("wquant", [P, 9, P], BF16)
        C.wscale = sb("wscale_keep", [P, 9])
        C.down_scale = sb("down_scale", [P, D])
        C.route = sb("route", [P, LEAVES])
        C.leaf = sb("leaf", [P, 2, D])
        C.peak = sb("peak", [P, 4])
        C.scale = sb("act_scale", [P, 4])
        C.clip = sb("clip", [P, 2])
        with nc.sbuf_tensor("w1_sb", [P, E, FC, P], F32) as w1:
            C.w1 = w1
            setup(nc, C, A)
            attention(nc, C, 0, C.row("bf0"))
            experts(nc, C, A)
        attention(nc, C, 1, C.row("bv1"))
        quantized_gated(nc, C)
        attention(nc, C, 2, C.row("bo2"))
        tree(nc, C)
        attention(nc, C, 3, C.row("bp3"))
        channel_mix(nc, C, A)


OUT = ("out", (P, NB, D))


def layout(inputs):
    i = {k: np.asarray(v) for k, v in inputs.items()}
    perm = np.arange(D).reshape(PART, PART, DH).transpose(1, 0, 2).reshape(-1)
    col = lambda b: b.reshape(-1, 1)
    a = {}
    for l, (q, k, v) in enumerate((("L0_xattn_Wq", "L0_xattn_Wk", "L0_xattn_Wv"), ("L1_xattn_wq", "L1_xattn_wk", "L1_xattn_wv"),
                                   ("L2_xattn_wq", "L2_xattn_wk", "L2_xattn_wv"))):
        a[f"wq{l}"], a[f"wk{l}"], a[f"wv{l}"] = i[q][:, perm], i[k][:, perm], i[v]
        q, k, v = (n.replace("W", "b").replace("_w", "_b") for n in (q, k, v))
        a[f"bq{l}"], a[f"bk{l}"], a[f"bv{l}"] = col(i[q][perm]), col(i[k][perm]), col(i[v])
    a["wq3"], a["wk3"], a["wv3"] = i["L3_xattn_w_attn"][:, perm], i["L3_xattn_w_vis"][:, perm], i["L3_xattn_w_vis"]
    a["bq3"], a["bk3"], a["bv3"] = (col(i["L3_xattn_b_attn"][perm]), col(i["L3_xattn_b_vis"][perm]), col(i["L3_xattn_b_vis"]))
    a["wo0"], a["wo2"], a["wo3"] = i["L0_xattn_Wf"], i["L2_xattn_wo"], i["L3_xattn_w_proj"]
    a["choice"] = i["L0_ffn_choice"].T

    def rows_in_chunks(w):
        w = np.concatenate([w, np.zeros((3 * P - I1, D), w.dtype)])
        return w.reshape(3, P, D).transpose(1, 0, 2).reshape(P, 3 * D)

    a["gate"], a["up"] = rows_in_chunks(i["L1_ffn_w_gate"]), rows_in_chunks(i["L1_ffn_w_up"])
    a["down"] = np.concatenate([i["L1_ffn_w_down"], np.zeros((D, 3 * P - I1), np.float32)], axis=1)
    a["tree_q"] = i["L2_ffn_Wq"]
    a["routers"] = np.concatenate([i["L2_ffn_routers"], np.zeros((1, D), np.float32)]).T
    a["leaves"], a["tree_out"] = i["L2_ffn_leaf_values"].T, i["L2_ffn_Wout_w"].T
    a["mix_r"], a["mix_k"], a["mix_v"] = i["L3_ffn_W_r"].T, i["L3_ffn_W_k"].T, i["L3_ffn_W_v"].T
    a["mu_r"], a["mu_k"] = col(i["L3_ffn_mu_r"]), col(i["L3_ffn_mu_k"])
    rows = {"bf0": i["L0_xattn_bf"], "bv1": i["L1_xattn_bv"], "bo2": i["L2_xattn_bo"], "bp3": i["L3_xattn_b_proj"],
            "tree_b": i["L2_ffn_Wout_b"], "clip_x": i["L1_ffn_clip_x"], "clip_down": i["L1_ffn_clip_down"]}
    return {
        "x": i["x"].transpose(1, 0, 2),
        "ctx": i["ctx_1024"].transpose(2, 0, 1),
        "pack": np.concatenate([a[n] for n in PACK], axis=1),
        "rows": np.concatenate([rows[n] for n in ROWS]).reshape(1, ROW_COLS),
        "lens": i["_lenS2"].reshape(1, NB),
        "mask": i["mask_1x1xSxS2_fk1"].reshape(P, TK),
        "w1": i["L0_ffn_W1"].reshape(E, D, FC, P).transpose(1, 0, 2, 3),
        "w2": i["L0_ffn_W2"].reshape(E, FC, P, D).transpose(2, 0, 1, 3),
    }


def kernel(**inputs):
    import concourse.bacc as bacc
    from concourse.bass_utils import run_bass_kernel_spmd

    nc = bacc.Bacc("TRN2", target_bir_lowering=False, num_devices=1)
    arrays = {f"in_{n}": np.ascontiguousarray(a) for n, a in layout(inputs).items()}
    A = {n[3:]: nc.dram_tensor(n, a.shape, mybir.dt.from_np(a.dtype), kind="ExternalInput").ap() for n, a in arrays.items()}
    A["out"] = nc.dram_tensor(OUT[0], OUT[1], F32, kind="ExternalOutput").ap()
    program(nc, A)
    r = run_bass_kernel_spmd(nc, [arrays], core_ids=[0])
    return np.ascontiguousarray(r.results[0][OUT[0]].transpose(1, 0, 2))
```
